# Optimizing a Trainium2 kernel written in Bass

```python
import numpy as np
import jax
import jax.numpy as jnp

def _softmax(x, axis=-1):
    return jax.nn.softmax(x, axis=axis)

def _gelu(x):
    return jax.nn.gelu(x, approximate=True)

def _silu(x):
    return jax.nn.silu(x)

def _sigmoid(x):
    return jax.nn.sigmoid(x)

def _layernorm(x, axis=-1, eps=1e-05):
    m = jnp.mean(x, axis=axis, keepdims=True)
    v = jnp.var(x, axis=axis, keepdims=True)
    return (x - m) / jnp.sqrt(v + eps)

def _scatter_add(tgt, idx, src, axis=0):
    return tgt.at[idx].add(src)

def _segment_sum(src, seg, n):
    return jax.ops.segment_sum(src, seg, n)
kernel_name = 'mk_lm_tower_d1_tok_ids768_r4_17db94'

def setup_inputs(seed: int=0):
    np.random.seed(seed)
    _w = jnp.asarray

    def _rec_inputs():
        import jax
        import jax.numpy as jnp
        _rk = jax.random.key(seed)
        x = jax.random.randint(jax.random.fold_in(_rk, 1), (16, 512), 0, 12564, jnp.int32)
        return x
    x = _rec_inputs()

    def _L0_tok_setup():
        import jax, jax.numpy as jnp
        import numpy as np
        D_MODEL = 192
        N_HEADS = 8
        D_TRACE = 64
        TRACE_LR = 0.1
        TRACE_DECAY = 0.99
        LN_EPS = 1e-05
        B, S, VOCAB = (8, 1024, 50257)

        def _ln(x, w, b):
            m = x.mean(-1, keepdims=True)
            v = ((x - m) ** 2).mean(-1, keepdims=True)
            return (x - m) / jnp.sqrt(v + LN_EPS) * w + b
        key = jax.random.key(seed)
        ks = jax.random.split(key, 6)
        return {'input_ids': jax.random.randint(ks[0], (B, S), 0, VOCAB), 'wte': jax.random.normal(ks[1], (VOCAB, D_MODEL), jnp.float32) * 0.02, 'W_proj': jax.random.normal(ks[2], (N_HEADS * D_TRACE, D_MODEL), jnp.float32) / np.float32(np.sqrt(D_MODEL)), 'ln_w': jnp.ones((D_MODEL,), jnp.float32), 'ln_b': jnp.zeros((D_MODEL,), jnp.float32), 'W_val': jax.random.normal(ks[3], (N_HEADS * D_TRACE, D_MODEL), jnp.float32) / np.float32(np.sqrt(D_MODEL)), 'W_out': jax.random.normal(ks[4], (D_MODEL, N_HEADS * D_TRACE), jnp.float32) / np.float32(np.sqrt(N_HEADS * D_TRACE)), 'trace0': jax.random.normal(ks[5], (N_HEADS, D_TRACE, D_TRACE), jnp.float32) * 0.01}
    _L0_tok_all = _L0_tok_setup()
    _L0_tok_in = {k: v for k, v in _L0_tok_all.items() if k in ('wte', 'W_proj', 'ln_w', 'ln_b', 'W_val', 'W_out', 'trace0')}
    del _L0_tok_all

    def _L0_attn_setup():
        import jax, jax.numpy as jnp
        import numpy as np
        N_HEADS = 12
        key = jax.random.key(seed)
        k1, k2, k3 = jax.random.split(key, 3)
        B, S, W = (8, 256, 192)
        x = jax.random.normal(k1, (B, S, W), dtype=jnp.float32)
        w_qkv = jax.random.normal(k2, (W, 3 * W), dtype=jnp.float32) * W ** (-0.5)
        w_out = jax.random.normal(k3, (W, W), dtype=jnp.float32) * W ** (-0.5)
        return {'x': x, 'w_qkv': w_qkv, 'w_out': w_out}
    _L0_attn_all = _L0_attn_setup()
    _L0_attn_in = {k: v for k, v in _L0_attn_all.items() if k in ('w_qkv', 'w_out')}
    del _L0_attn_all

    def _L0_ffn_setup():
        import math
        import jax, jax.numpy as jnp
        import numpy as np
        EMBED_CHOICES = [96, 144, 192]
        RATIO_CHOICES = [2, 3, 4]
        E_MAX = 192
        H_MAX = 768

        def new_gelu(x):
            c = math.sqrt(2.0 / math.pi)
            return 0.5 * x * (1.0 + jnp.tanh(c * (x + 0.044715 * x * x * x)))

        def _mixed_coeffs(alpha_e, alpha_r):
            h_idx = jnp.arange(H_MAX)
            d_idx = jnp.arange(E_MAX)
            C0 = jnp.zeros((H_MAX, E_MAX), jnp.float32)
            c0b = jnp.zeros((H_MAX,), jnp.float32)
            C1 = jnp.zeros((E_MAX, H_MAX), jnp.float32)
            c1b = jnp.zeros((E_MAX,), jnp.float32)
            for i, e in enumerate(EMBED_CHOICES):
                m_in = (d_idx < e).astype(jnp.float32)
                for j, r in enumerate(RATIO_CHOICES):
                    a = alpha_e[i] * alpha_r[j]
                    m_out = (h_idx < r * e).astype(jnp.float32)
                    C0 = C0 + a * (m_out[:, None] * m_in[None, :])
                    c0b = c0b + a * m_out
                    C1 = C1 + a * (m_in[:, None] * m_out[None, :])
                    c1b = c1b + a * m_in
            return (C0, c0b, C1, c1b)
        key = jax.random.key(seed)
        ks = jax.random.split(key, 6)
        x = jax.random.normal(ks[0], (8, 512, E_MAX), jnp.float32)
        w_fc = jax.random.normal(ks[1], (H_MAX, E_MAX), jnp.float32) * 0.02
        b_fc = jnp.zeros((H_MAX,), jnp.float32)
        w_proj = jax.random.normal(ks[2], (E_MAX, H_MAX), jnp.float32) * 0.02
        b_proj = jnp.zeros((E_MAX,), jnp.float32)
        alpha_e = jax.nn.softmax(jax.random.normal(ks[3], (3,), jnp.float32))
        alpha_r = jax.nn.softmax(jax.random.normal(ks[4], (3,), jnp.float32))
        return {'x': x, 'w_fc': w_fc, 'b_fc': b_fc, 'w_proj': w_proj, 'b_proj': b_proj, 'alpha_e': alpha_e, 'alpha_r': alpha_r}
    _L0_ffn_all = _L0_ffn_setup()
    _L0_ffn_in = {k: v for k, v in _L0_ffn_all.items() if k in ('w_fc', 'b_fc', 'w_proj', 'b_proj', 'alpha_e', 'alpha_r')}
    del _L0_ffn_all
    return {'x': x, 'L0_tok_wte': _L0_tok_in['wte'], 'L0_tok_W_proj': _L0_tok_in['W_proj'], 'L0_tok_ln_w': _L0_tok_in['ln_w'], 'L0_tok_ln_b': _L0_tok_in['ln_b'], 'L0_tok_W_val': _L0_tok_in['W_val'], 'L0_tok_W_out': _L0_tok_in['W_out'], 'L0_tok_trace0': _L0_tok_in['trace0'], 'L0_attn_w_qkv': _L0_attn_in['w_qkv'], 'L0_attn_w_out': _L0_attn_in['w_out'], 'L0_ffn_w_fc': _L0_ffn_in['w_fc'], 'L0_ffn_b_fc': _L0_ffn_in['b_fc'], 'L0_ffn_w_proj': _L0_ffn_in['w_proj'], 'L0_ffn_b_proj': _L0_ffn_in['b_proj'], 'L0_ffn_alpha_e': _L0_ffn_in['alpha_e'], 'L0_ffn_alpha_r': _L0_ffn_in['alpha_r']}

def reference(x, L0_tok_wte, L0_tok_W_proj, L0_tok_ln_w, L0_tok_ln_b, L0_tok_W_val, L0_tok_W_out, L0_tok_trace0, L0_attn_w_qkv, L0_attn_w_out, L0_ffn_w_fc, L0_ffn_b_fc, L0_ffn_w_proj, L0_ffn_b_proj, L0_ffn_alpha_e, L0_ffn_alpha_r):
    import jax
    import jax.numpy as jnp

    def _L0_tok_ref(input_ids, wte, W_proj, ln_w, ln_b, W_val, W_out, trace0):
        import jax, jax.numpy as jnp
        import numpy as np
        D_MODEL = 192
        N_HEADS = 8
        D_TRACE = 64
        TRACE_LR = 0.1
        TRACE_DECAY = 0.99
        LN_EPS = 1e-05
        B, S, VOCAB = (8, 1024, 50257)

        def _ln(x, w, b):
            m = x.mean(-1, keepdims=True)
            v = ((x - m) ** 2).mean(-1, keepdims=True)
            return (x - m) / jnp.sqrt(v + LN_EPS) * w + b
        B_, S_ = input_ids.shape
        tok = wte[input_ids]
        Q = _ln(tok, ln_w, ln_b) @ W_proj.T
        V = tok @ W_val.T
        Q = Q.reshape(B_, S_, N_HEADS, D_TRACE).transpose(0, 2, 1, 3)
        V = V.reshape(B_, S_, N_HEADS, D_TRACE).transpose(0, 2, 1, 3)
        Q_store = Q[:, :, :-2, :]
        V_store = V[:, :, 2:, :]
        denom = jnp.float32(B_ * (S_ - 2))
        upd = jnp.einsum('bhip,bhiq->hpq', Q_store, V_store) / denom
        trace = TRACE_DECAY * trace0 + TRACE_LR * upd
        Q_addr = jnp.concatenate([jnp.zeros_like(Q[:, :, :1, :]), Q[:, :, :-1, :]], axis=2)
        V_ret = jnp.einsum('bhsp,hpq->bhsq', Q_addr, trace)
        V_flat = V_ret.transpose(0, 2, 1, 3).reshape(B_, S_, N_HEADS * D_TRACE)
        return V_flat @ W_out.T

    def _L0_attn_ref(x, w_qkv, w_out):
        import jax, jax.numpy as jnp
        import numpy as np
        N_HEADS = 12
        B, S, W = x.shape
        H = N_HEADS
        D = W // H
        scale = W ** (-0.5)
        qkv = x @ w_qkv
        q, k, v = jnp.split(qkv, 3, axis=2)
        q = q.reshape(B, S, H, D)
        k = k.reshape(B, S, H, D)
        attn_score = jnp.einsum('binh,bjnh->bijn', q, k) * scale
        attn_weight = jax.nn.softmax(attn_score, axis=2)
        out = jnp.einsum('bijn,bjnh->binh', attn_weight, k)
        out = out.reshape(B, S, W)
        return out @ w_out

    def _L0_ffn_ref(x, w_fc, b_fc, w_proj, b_proj, alpha_e, alpha_r):
        import math
        import jax, jax.numpy as jnp
        import numpy as np
        EMBED_CHOICES = [96, 144, 192]
        RATIO_CHOICES = [2, 3, 4]
        E_MAX = 192
        H_MAX = 768

        def new_gelu(x):
            c = math.sqrt(2.0 / math.pi)
            return 0.5 * x * (1.0 + jnp.tanh(c * (x + 0.044715 * x * x * x)))

        def _mixed_coeffs(alpha_e, alpha_r):
            h_idx = jnp.arange(H_MAX)
            d_idx = jnp.arange(E_MAX)
            C0 = jnp.zeros((H_MAX, E_MAX), jnp.float32)
            c0b = jnp.zeros((H_MAX,), jnp.float32)
            C1 = jnp.zeros((E_MAX, H_MAX), jnp.float32)
            c1b = jnp.zeros((E_MAX,), jnp.float32)
            for i, e in enumerate(EMBED_CHOICES):
                m_in = (d_idx < e).astype(jnp.float32)
                for j, r in enumerate(RATIO_CHOICES):
                    a = alpha_e[i] * alpha_r[j]
                    m_out = (h_idx < r * e).astype(jnp.float32)
                    C0 = C0 + a * (m_out[:, None] * m_in[None, :])
                    c0b = c0b + a * m_out
                    C1 = C1 + a * (m_in[:, None] * m_out[None, :])
                    c1b = c1b + a * m_in
            return (C0, c0b, C1, c1b)
        C0, c0b, C1, c1b = _mixed_coeffs(alpha_e, alpha_r)
        W0 = w_fc * C0
        b0 = b_fc * c0b
        h = jnp.einsum('bte,he->bth', x, W0) + b0
        h = new_gelu(h)
        W1 = w_proj * C1
        b1 = b_proj * c1b
        out = jnp.einsum('bth,eh->bte', h, W1) + b1
        return out
    h = _L0_tok_ref(x, L0_tok_wte, L0_tok_W_proj, L0_tok_ln_w, L0_tok_ln_b, L0_tok_W_val, L0_tok_W_out, L0_tok_trace0)
    h = h + _L0_attn_ref(_layernorm(h, axis=-1), L0_attn_w_qkv, L0_attn_w_out)
    h = h + _L0_ffn_ref(_layernorm(h, axis=-1), L0_ffn_w_fc, L0_ffn_b_fc, L0_ffn_w_proj, L0_ffn_b_proj, L0_ffn_alpha_e, L0_ffn_alpha_r)
    return h

_drawn_inputs = setup_inputs


def setup_inputs(seed=0):
    import zlib

    import numpy as np

    out = dict(_drawn_inputs(seed))
    spreads = {'L0_tok_ln_w': (1.0, 0.2),
     'L0_tok_ln_b': (0.0, 0.1),
     'L0_ffn_b_fc': (0.0, 0.1),
     'L0_ffn_b_proj': (0.0, 0.1)}
    factors = {'L0_tok_W_val': 8.0}
    for name, (base, spread) in spreads.items():
        noise = np.random.default_rng([zlib.crc32(name.encode()), seed]).standard_normal(out[name].shape)
        drawn = base * np.exp(spread * noise) if base else spread * noise
        out[name] = jnp.asarray(drawn.astype(out[name].dtype))
    for name, factor in factors.items():
        out[name] = (out[name] * factor).astype(out[name].dtype)
    return out
```

```python
from contextlib import ExitStack

import numpy as np
import concourse.bass as bass
from concourse import mybir

F32 = mybir.dt.float32
BF16 = mybir.dt.bfloat16
I32 = mybir.dt.int32
ACT = mybir.ActivationFunctionType
ALU = mybir.AluOpType
AX_X = mybir.AxisListType.X

P = 128
B, S, D = 16, 512, 192
C = D // 2
CH = 8
TS = S // CH
LAG = 2
NG = TS // 4
TH, TD = 8, 64
NH, HD = 12, 16
NT = S // P
HID, HC = 768, 6
EPS = 1e-5
DECAY = 0.99
UPDATE = 0.1 / (B * (S - LAG))
SCALE = float(D) ** -0.5
EMBED = [96, 144, 192]
RATIO = [2, 3, 4]
QPARTS = [0, 0, 1, 0, 1, 2]
KPARTS = [0, 1, 0, 2, 1, 0]
ST = 6 * HD
STEPS = 24
PAIRS_AT = [s for s in range(1, 21)] + [6, 7, 14, 18]
PAIRS_AT.sort()


def wait(eng, sem, value):
    if not (isinstance(value, int) and value <= 0):
        eng.wait_ge(sem, value)


def wait_apart(eng, sem, value, passed):
    wait(eng, sem, value)
    if not isinstance(value, int):
        eng.sem_inc(passed, 1)


def tower(nc, ids, wte, wpT, wvT, wpN, woT, t0T, lnw, lnb, wqk, wout, w0T, bfc, w1T, bproj,
          al_e, al_r, out):
    lnx_d = nc.dram_tensor("lnx_d", [B, C, 2, S], F32).ap()
    parts_d = nc.dram_tensor("parts_d", [3, 4 * C, S], BF16).ap()
    h0_d = nc.dram_tensor("h0_d", [B, P, NT * D], F32).ap()
    y_d = nc.dram_tensor("y_d", [B, P, NT * D], F32).ap()

    with ExitStack() as top:
        def sb(name, shape, dt, ctx=top):
            return ctx.enter_context(nc.sbuf_tensor(name, shape, dt))

        def sem(name):
            return top.enter_context(nc.semaphore(name))

        ps = top.enter_context(nc.psum_tensor("ps", [P, 8, 512], F32))
        ident = sb("ident", [P, P], F32)
        M = sb("M", [C, 2, D], F32)
        w0 = sb("w0", [C, 2, HID], F32)
        w1 = sb("w1", [P, HC, D], F32)
        b0 = sb("b0", [P, HC], F32)
        b1 = sb("b1", [P, D], F32)
        wqk_s = sb("wqk_s", [C, 2, 2 * D], F32)
        wout_s = sb("wout_s", [P, 3, D], F32)
        half = sb("half", [P, 4], F32)
        wide = sb("wide", [P, 2 * B * S], F32)

        passed = sem("passed")
        d_const = sem("d_const")
        d_ffn = sem("d_ffn")
        g_const = sem("g_const")
        d_lnx = [sem(f"d_lnx{k}") for k in range(4)]

        with ExitStack() as ph:
            tok = sb("tok", [P, TS + LAG, D], F32, ph)
            xn = sb("xn", [P, 2, 4, D + 2], F32, ph)
            idx = sb("idx", [P, TS + LAG], I32, ph)
            keeps = sb("keeps", [P, B], F32, ph)
            keep = sb("keep", [P, 1], F32, ph)
            st = sb("st", [P, 4, 6], F32, ph)
            mv = sb("mv", [P, 4, 2], F32, ph)
            ve = sb("ve", [P, 4], F32, ph)
            rstd = sb("rstd", [P, 4], F32, ph)
            zero = sb("zero", [P, D], F32, ph)
            wp = sb("wp", [C + 1, 2, TH * TD], F32, ph)
            wv = sb("wv", [C, 2, TH * TD], F32, ph)
            wpn = sb("wpn", [TD, TH, D], F32, ph)
            wo = sb("wo", [TD, TH, D], F32, ph)
            t0 = sb("t0", [TD, TH, TD], F32, ph)
            lw = sb("lw", [C, 2], F32, ph)
            lb = sb("lb", [C, 2], F32, ph)
            bcol = sb("bcol", [C, 2, C + 1], F32, ph)
            G = sb("G", [C + 1, 2, D], F32, ph)
            U = sb("U", [C, 2, TH * TD], F32, ph)
            trace = sb("trace", [TD, TH, TD], F32, ph)
            X = sb("X", [TD, TH, D], F32, ph)
            ae = sb("ae", [P, 3], F32, ph)
            ar = sb("ar", [P, 3], F32, ph)
            a = sb("a", [P, 9], F32, ph)
            hm = sb("hm", [P, 9, HC], F32, ph)
            em = sb("em", [C, 1], F32, ph)
            hma = sb("hma", [P, 9, HC], F32, ph)
            ema = sb("ema", [C, 9], F32, ph)
            c0 = sb("c0", [C, 2, HID], F32, ph)
            c1 = sb("c1", [P, HC, D], F32, ph)
            c0b = sb("c0b", [P, HC], F32, ph)
            c1b = sb("c1b", [P, D], F32, ph)

            gath = [sem(f"gath{k}") for k in range(4)]
            gath_tail = sem("gath_tail")
            d_idx = sem("d_idx")
            v_st = sem("v_st")
            v_ag = sem("v_ag")
            v_var = sem("v_var")
            p_rstd = sem("p_rstd")
            v_xn = sem("v_xn")
            t_tr = sem("t_tr")
            a_ln = sem("a_ln")
            t_G = sem("t_G")
            v_ch = sem("v_ch")
            v_bcol = sem("v_bcol")
            t_bw = sem("t_bw")
            v_wp = sem("v_wp")
            t_m = sem("t_m")
            c_m = sem("c_m")

            lnx = wide[0:C, :].rearrange("p (c n) -> p c n", c=2)
            tr = [[ps[0:C, 2 * k + c, :].rearrange("p (t q) -> p t q", t=4) for c in range(2)] for k in range(2)]
            G_ps = [ps[0:C, 4, 0:D], ps[0:C + 1, 5, 0:D]]
            trace_ps = ps[0:TD, 6, :].rearrange("p (h q) -> p h q", h=TH)
            X_ps = ps[0:TD, 0:4, 0:2 * D]
            M_ps = ps[0:C, 4:6, 0:D]

            def tile_of(t):
                return tok[:, bass.ds(t, 1), :].rearrange("p o f -> p (o f)")

            block = ph.enter_context(nc.Block())

            @block.sync
            def _(sp):
                sp.dma_start(idx[:, :], ids).then_inc(d_idx, 16)
                for to, of in ((lw[:, :], lnw), (lb[:, :], lnb), (wp[0:C, :, :], wpT), (wv[:, :, :], wvT),
                               (wpn[:, :, :], wpN), (wo[:, :, :], woT), (t0[:, :, :], t0T), (wqk_s[:, :, :], wqk)):
                    sp.dma_start(to, of).then_inc(d_const, 16)
                for to, of in ((w0[:, :, :], w0T), (w1[:, :, :], w1T), (b0[:, :], bfc),
                               (b1[:, :], bproj.to_broadcast([P, D])), (ae[:, :], al_e.to_broadcast([P, 3])),
                               (ar[:, :], al_r.to_broadcast([P, 3]))):
                    sp.dma_start(to, of).then_inc(d_ffn, 16)
                sp.wait_ge(g_const, 1)
                for h in range(NH):
                    r = 32 * (h % 4)
                    sp.dma_start(wout_s[r:r + HD, h // 4, :], wout[h * HD:(h + 1) * HD, :]).then_inc(d_const, 16)
                sp.wait_ge(a_ln, 2 * NG)
                for b in range(B):
                    sp.dma_start(lnx_d[b, :, :, :], lnx[:, :, b * S:(b + 1) * S]).then_inc(d_lnx[b // 4], 16)

            @block.gpsimd
            def _(pool):
                pool.memset(wout_s[:, :, :], 0.0).then_inc(g_const, 1)
                pool.wait_ge(d_idx, 16)

                def gather(t, done):
                    pool.indirect_dma_start(out=tok[:, t, :], out_offset=None, in_=wte,
                                            in_offset=bass.IndirectOffsetOnAxis(ap=idx[:, t:t + 1], axis=0)
                                            ).then_inc(done, 16)

                for t in range(12):
                    gather(t, gath[t // 4])
                pool.memset(half[:, :], -0.5).then_inc(g_const, 1)
                pool.memset(ident[:, :], 0.0).then_inc(g_const, 1)
                pool.memset(keeps[:, :], 1.0).then_inc(g_const, 1)
                pool.memset(hm[:, :, :], 1.0).then_inc(g_const, 1)
                pool.memset(em[:, :], 1.0).then_inc(g_const, 1)
                pool.wait_ge(g_const, 6)
                pool.affine_select(out=ident[:, :], in_=ident[:, :], compare_op=ALU.not_equal, fill=1.0,
                                   base=0, pattern=[[-1, P]], channel_multiplier=1).then_inc(g_const, 1)
                pool.affine_select(out=keeps[:, :], in_=keeps[:, :], compare_op=ALU.not_equal, fill=0.0,
                                   base=-(CH - 1), pattern=[[-CH, B]], channel_multiplier=1).then_inc(g_const, 1)
                pool.affine_select(out=em[:, :], in_=em[:, :], compare_op=ALU.is_ge, fill=0.0,
                                   base=EMBED[1] - C - 1, pattern=[[0, 1]], channel_multiplier=-1).then_inc(g_const, 1)
                for ij in range(9):
                    pool.affine_select(out=hm[:, ij, :], in_=hm[:, ij, :], compare_op=ALU.is_ge, fill=0.0,
                                       base=RATIO[ij % 3] * EMBED[ij // 3] - 1, pattern=[[-P, HC]],
                                       channel_multiplier=-1).then_inc(g_const, 1)
                for g in range(NG):
                    if g + 3 < NG:
                        if g + 3 >= 4:
                            pool.wait_ge(gath[(g + 3) % 4], 64 * ((g + 3) // 4))
                        for t in range(4 * (g + 3), 4 * (g + 4)):
                            gather(t, gath[(g + 3) % 4])
                    if g == NG - 4:
                        for t in range(TS, TS + LAG):
                            gather(t, gath_tail)
                    pool.wait_ge(v_var, g + 1)
                    pool.tensor_tensor(rstd[:, :], ve[:, :], half[:, :], ALU.pow).then_inc(p_rstd, 1)

            @block.scalar
            def _(act):
                act.wait_ge(d_const, 16 * 20)
                with act.Fori(0, NG // 2) as it:
                    for k in range(2):
                        g = 2 * it + k
                        act.wait_ge(t_tr, g + 1)
                        for c in range(2):
                            view = lnx[:, c, :].rearrange("p (q t) -> p t q", t=TS)
                            act.activation(view[:, bass.ds(4 * g, 4), :], tr[k][c], ACT.Identity,
                                           scale=lw[:, c:c + 1], bias=lb[:, c:c + 1]).then_inc(a_ln, 1)
                act.wait_ge(t_m, 1)
                for i in range(2):
                    act.copy(G[0:C + i, i, :], G_ps[i]).then_inc(c_m, 1)
                act.wait_ge(t_m, 2)
                for i in range(2):
                    act.copy(U[:, i, :], ps[0:C, i, :]).then_inc(c_m, 1)
                act.wait_ge(t_m, 4)
                act.copy(X[:, :, :].rearrange("p (i h) e -> p i (h e)", h=2), X_ps).then_inc(c_m, 1)
                act.wait_ge(t_m, 5)
                act.copy(M[:, :, :], M_ps).then_inc(c_m, 1)

            @block.vector
            def _(dve):
                chain = [0]

                def step(ins):
                    chain[0] += 1
                    ins.then_inc(v_ch, 1)
                    dve.wait_ge(v_ch, chain[0])

                dve.memset(xn[:, :, :, D:D + 1], 1.0).then_inc(v_ch, 1)
                dve.memset(zero[:, :], 0.0).then_inc(v_ch, 1)
                dve.memset(bcol[:, :, :], 0.0).then_inc(v_ch, 1)
                chain[0] = 3
                dve.wait_ge(v_ch, 3)
                dve.wait_ge(d_const, 16 * 20)
                dve.tensor_copy(bcol[:, :, C:C + 1], lb[:, :].rearrange("p (c o) -> p c o", o=1)).then_inc(v_bcol, 1)
                dve.wait_ge(t_bw, 1)
                for c in range(2):
                    dve.tensor_scalar(wp[0:C, c, :], wp[0:C, c, :], lw[:, c:c + 1], None, ALU.mult).then_inc(v_wp, 1)
                dve.tensor_copy(wp[C:C + 1, 1, :], ps[C:C + 1, 6, :]).then_inc(v_wp, 1)
                dve.tensor_scalar(t0[:, :, :], t0[:, :, :], DECAY, None, ALU.mult).then_inc(v_wp, 1)

                dve.wait_ge(d_ffn, 16 * 6)
                dve.wait_ge(g_const, 18)
                for i in range(3):
                    step(dve.tensor_scalar(a[:, 3 * i:3 * i + 3], ar[:, :], ae[:, i:i + 1], None, ALU.mult))
                step(dve.memset(c0[:, :, :], 0.0))
                step(dve.memset(c1[:, :, :], 0.0))
                step(dve.memset(c0b[:, :], 0.0))
                step(dve.memset(c1b[:, :], 0.0))
                step(dve.tensor_scalar(ema[:, :], a[0:C, :], em[:, 0:1], None, ALU.mult))
                for ij in range(9):
                    step(dve.tensor_scalar(hma[:, ij, :], hm[:, ij, :], a[:, ij:ij + 1], None, ALU.mult))
                for ij in range(9):
                    i, j = ij // 3, ij % 3
                    e, h = EMBED[i], RATIO[j] * EMBED[i]
                    dve.tensor_scalar(c0[:, 0, 0:h], c0[:, 0, 0:h], a[0:C, ij:ij + 1], None, ALU.add)
                    if i:
                        upper = a[0:C, ij:ij + 1] if i == 2 else ema[:, ij:ij + 1]
                        dve.tensor_scalar(c0[:, 1, 0:h], c0[:, 1, 0:h], upper, None, ALU.add)
                    for k in range((h + P - 1) // P):
                        dve.tensor_scalar(c1[:, k, 0:e], c1[:, k, 0:e], hma[:, ij, k:k + 1], None, ALU.add)
                    dve.tensor_tensor(c0b[:, :], c0b[:, :], hma[:, ij, :], ALU.add)
                    step(dve.tensor_scalar(c1b[:, 0:e], c1b[:, 0:e], a[:, ij:ij + 1], None, ALU.add))
                step(dve.tensor_tensor(w0[:, :, :], w0[:, :, :], c0[:, :, :], ALU.mult))
                step(dve.tensor_tensor(w1[:, :, :], w1[:, :, :], c1[:, :, :], ALU.mult))
                step(dve.tensor_tensor(b0[:, :], b0[:, :], c0b[:, :], ALU.mult))
                step(dve.tensor_tensor(b1[:, :], b1[:, :], c1b[:, :], ALU.mult))

                with dve.Fori(0, NG // 4) as it:
                    for k in range(4):
                        g = 4 * it + k
                        dve.wait_ge(gath[k], 64 * (it + 1))
                        for j in range(4):
                            dve.bn_stats(st[:, j, :], tile_of(4 * g + j)).then_inc(v_st, 1)
                        wait_apart(dve, v_st, 4 * g + 4, passed)
                        for j in range(4):
                            dve.bn_aggr(mv[:, j, :], st[:, j, :]).then_inc(v_ag, 1)
                        dve.wait_ge(v_ag, 4 * g + 4)
                        dve.tensor_scalar(ve[:, :], mv[:, :, 1], EPS, None, ALU.add).then_inc(v_var, 1)
                        dve.wait_ge(t_G, g + 1)
                        dve.wait_ge(p_rstd, g + 1)
                        for j in range(4):
                            dve.tensor_scalar(xn[:, k % 2, j, 0:D], tile_of(4 * g + j), mv[:, j, 0:1],
                                              rstd[:, j:j + 1], ALU.subtract, ALU.mult).then_inc(v_xn, 1)

                dve.tensor_reduce(keep[:, :], keeps[:, :], AX_X, ALU.min).then_inc(v_ch, 1)
                chain[0] += 1
                dve.wait_ge(v_ch, chain[0])
                dve.wait_ge(gath_tail, 16 * LAG)
                dve.tensor_scalar(tok[:, TS:TS + LAG, :], tok[:, TS:TS + LAG, :], keep[:, 0:1], None,
                                  ALU.mult).then_inc(v_ag, 4)
                dve.wait_ge(t_m, 3)
                dve.scalar_tensor_tensor(out=trace[:, :, :], in0=trace_ps, scalar=UPDATE, in1=t0[:, :, :],
                                         op0=ALU.mult, op1=ALU.add).then_inc(c_m, 1)

            @block.tensor
            def _(pe):
                pe.wait_ge(v_bcol, 1)
                for c in range(2):
                    last = pe.matmul(ps[0:C + 1, 6, :], bcol[:, c, :], wp[0:C, c, :], start=(c == 0), stop=(c == 1))
                last.then_inc(t_bw, 1)
                pe.matmul(G_ps[0], zero[:, 0:C], zero[:, :], start=True, stop=False).then_inc(t_G, 1)
                pe.matmul(G_ps[1], zero[:, 0:C + 1], zero[:, :], start=True, stop=False).then_inc(t_G, 1)
                pe.wait_ge(g_const, 7)

                def group(g, k):
                    pe.wait_ge(v_xn, 4 * g + 4)
                    wait(pe, a_ln, 2 * (g - 1))
                    for c in range(2):
                        for j in range(4):
                            last = pe.transpose(tr[k][c][:, j, :], xn[:, k, j, c * C:(c + 1) * C], ident[:, :])
                    last.then_inc(t_tr, 1)
                    pe.wait_ge(v_ag, 4 * (g + 2))
                    for j in range(4):
                        later = tile_of(4 * g + j + LAG)
                        pe.matmul(G_ps[0], xn[:, k, j, 0:C], later, start=False, stop=False)
                        last = pe.matmul(G_ps[1], xn[:, k, j, C:D + 1], later, start=False, stop=False)
                    last.then_inc(t_G, 1)

                group(0, 0)
                group(1, 1)
                with pe.Fori(1, NG // 2) as it:
                    group(2 * it, 0)
                    group(2 * it + 1, 1)
                pe.matmul(G_ps[0], zero[:, 0:C], zero[:, :], start=False, stop=True)
                pe.matmul(G_ps[1], zero[:, 0:C + 1], zero[:, :], start=False, stop=True).then_inc(t_m, 1)
                pe.wait_ge(c_m, 2)
                pe.wait_ge(v_wp, 4)
                pe.wait_ge(a_ln, 2 * NG)
                for i in range(2):
                    for c in range(2):
                        last = pe.matmul(ps[0:C, i, :], G[0:C + c, c, i * C:(i + 1) * C], wp[0:C + c, c, :],
                                         start=(c == 0), stop=(c == 1))
                last.then_inc(t_m, 1)
                pe.wait_ge(c_m, 4)
                for h in range(TH):
                    for c in range(2):
                        last = pe.matmul(trace_ps[:, h, :], wv[:, c, h * TD:(h + 1) * TD],
                                         U[:, c, h * TD:(h + 1) * TD], start=(c == 0), stop=(c == 1))
                last.then_inc(t_m, 1)
                pe.wait_ge(c_m, 5)
                for h in range(TH):
                    last = pe.matmul(X_ps[:, h // 2, D * (h % 2):D * (h % 2) + D], trace[:, h, :], wo[:, h, :],
                                     start=True, stop=True)
                last.then_inc(t_m, 1)
                pe.wait_ge(c_m, 6)
                for i in range(2):
                    for h in range(TH):
                        last = pe.matmul(M_ps[:, i, :], wpn[:, h, i * C:(i + 1) * C], X[:, h, :],
                                         start=(h == 0), stop=(h == TH - 1))
                last.then_inc(t_m, 1)

        with ExitStack() as ph:
            lnxb = sb("lnxb", [C, 2, S], F32, ph)
            h0 = sb("h0", [P, NT, D], F32, ph)
            z = sb("z", [P, NT, D], F32, ph)
            st2 = sb("st2", [P, NT, 6], F32, ph)
            mv2 = sb("mv2", [P, NT, 2], F32, ph)
            ve2 = sb("ve2", [P, NT], F32, ph)
            rstd2 = sb("rstd2", [P, NT], F32, ph)
            zT = sb("zT", [C, 2, S], F32, ph)
            x = sb("x", [C, 4, S], F32, ph)
            rest = sb("rest", [C, 4, S], F32, ph)
            part = [sb(f"part{r}", [C, 4, S], BF16, ph) for r in range(3)]
            kaug = [sb(f"kaug{k}", [P, NT, NH, 2 * HD], F32, ph) for k in range(2)]
            mx = sb("mx", [P, NT, NH], F32, ph)
            mrow = sb("mrow", [NH, 2, S], BF16, ph)
            sums = sb("sums", [P, S], F32, ph)
            recip = sb("recip", [P, S], F32, ph)
            oT = sb("oT", [P, 3, S], F32, ph)
            y = sb("y", [P, NT, D], F32, ph)
            q_even = sb("q_even", [P, NH, S], BF16, ph)
            k_even = sb("k_even", [P, NH, S], BF16, ph)
            E = wide[:, 0:16 * S].rearrange("p (u j i n) -> p u j i n", u=2, j=4, i=2)
            odd = wide[:, 16 * S:16 * S + NH * S].bitcast(BF16).rearrange("p (a h n) -> p a h n", a=2, h=NH)
            qs = [q_even[:, :, :], odd[:, 0, :, :]]
            ks = [k_even[:, :, :], odd[:, 1, :, :]]
            ROWS = ST + 2

            g_ones = sem("g_ones")
            d_x = sem("d_x")
            d_h0 = sem("d_h0")
            d_pt = sem("d_pt")
            d_st = [sem(f"d_st{g}") for g in range(3)]
            d_m = sem("d_m")
            d_y = sem("d_y")
            t_h0, a_h0 = sem("t_h0"), sem("a_h0")
            v_s2, v_a2, v_v2, p_r2 = sem("v_s2"), sem("v_a2"), sem("v_v2"), sem("p_r2")
            v_z = sem("v_z")
            t_zt, a_zt = sem("t_zt"), sem("a_zt")
            t_pr, a_x = sem("t_pr"), sem("a_x")
            v_hi, p_rest, v_mid, p_lo = sem("v_hi"), sem("p_rest"), sem("v_mid"), sem("p_lo")
            t_kt, a_kt = sem("t_kt"), sem("a_kt")
            t_mx, v_mx = sem("t_mx"), sem("v_mx")
            t_mt = sem("t_mt")
            v_mh, v_m = sem("v_mh"), sem("v_m")
            t_qk, a_exp = sem("t_qk"), sem("a_exp")
            t_pv = sem("t_pv")
            v_sh, v_rc, v_nm = sem("v_sh"), sem("v_rc"), sem("v_nm")
            t_op, a_y = sem("t_op"), sem("a_y")
            mb = ps[:, 7, :]

            block = ph.enter_context(nc.Block())

            @block.sync
            def _(sp):
                def load_x(n):
                    wait_apart(sp, t_h0, 2 * n, passed)
                    sp.dma_start(lnxb[:, :, 1:S], lnx_d[bass.ds(n, 1), :, :, 0:S - 1].rearrange("o p c t -> (o p) c t")
                                 ).then_inc(d_x, 16)

                def store_h0(n):
                    wait_apart(sp, a_h0, 2 * n + 2, passed)
                    sp.dma_start(h0_d[bass.ds(n, 1), :, :].rearrange("o p m -> (o p) m"),
                                 h0[:, :, :].rearrange("p t e -> p (t e)")).then_inc(d_h0, 16)

                def store_parts(n):
                    for g in range(3):
                        wait_apart(sp, d_st[g], 192 * n, passed)
                    for r, ready in enumerate((v_hi, v_mid, p_lo)):
                        sp.wait_ge(ready, n + 1)
                        sp.dma_start(parts_d[r, :, :].rearrange("(c p) t -> p c t", p=C),
                                     part[r][:, :, :]).then_inc(d_pt, 16)

                def load_stacks(n, par, g):
                    wait_apart(sp, d_pt, 48 * n + 48, passed)
                    wait(sp, t_qk, STEPS * (n - 2) + 8 * (g + 1))
                    for r in range(6):
                        for which, parts, stack in ((0, QPARTS, qs[par]), (1, KPARTS, ks[par])):
                            rows = parts_d[parts[r], which * D + 64 * g:which * D + 64 * (g + 1), :]
                            sp.dma_start(stack[HD * r:HD * (r + 1), 4 * g:4 * g + 4, :],
                                         rows.rearrange("(h d) t -> d h t", d=HD)).then_inc(d_st[g], 16)

                def load_max(n, par):
                    sp.wait_ge(v_m, n + 1)
                    wait(sp, t_qk, STEPS * (n - 1))
                    for r in range(2):
                        sp.dma_start(qs[par][ST + r:ST + r + 1, :, :], mrow[:, r, :]).then_inc(d_m, 16)

                def store_y(n):
                    wait_apart(sp, a_y, 2 * n + 2, passed)
                    sp.dma_start(y_d[bass.ds(n, 1), :, :].rearrange("o p m -> (o p) m"),
                                 y[:, :, :].rearrange("p t e -> p (t e)")).then_inc(d_y, 16)

                def sequence(b, par, first=False, front=True, last=False):
                    if front:
                        load_x(b + 2)
                        store_h0(b + 2)
                    if not first:
                        store_y(b - 1)
                    if front:
                        store_parts(b + 2)
                        load_stacks(b + 2, par, 0)
                        load_stacks(b + 2, par, 1)
                    if not last:
                        load_max(b + 1, 1 - par)
                    if front:
                        load_stacks(b + 2, par, 2)

                sp.wait_ge(g_ones, 1)
                sp.wait_ge(d_lnx[0], 64)
                load_x(0)
                store_h0(0)
                load_x(1)
                store_parts(0)
                for g in range(3):
                    load_stacks(0, 0, g)
                store_h0(1)
                store_parts(1)
                for k in range(1, 4):
                    sp.wait_ge(d_lnx[k], 64)
                for g in range(3):
                    load_stacks(1, 1, g)
                load_max(0, 0)
                sequence(0, 0, first=True)
                sequence(1, 1)
                with sp.Fori(1, B // 2 - 1) as it:
                    sequence(2 * it, 0)
                    sequence(2 * it + 1, 1)
                sequence(B - 2, 0, front=False)
                sequence(B - 1, 1, front=False, last=True)
                store_y(B - 1)
                sp.wait_ge(d_h0, 16 * B)
                sp.wait_ge(d_y, 16 * B)

            @block.gpsimd
            def _(pool):
                def norm(n):
                    pool.wait_ge(v_v2, n + 1)
                    pool.tensor_tensor(rstd2[:, :], ve2[:, :], half[:, :], ALU.pow).then_inc(p_r2, 1)

                def split(n):
                    pool.wait_ge(v_hi, n + 1)
                    wait(pool, v_mid, n)
                    pool.tensor_tensor(rest[:, :, :], x[:, :, :], part[0][:, :, :], ALU.subtract).then_inc(p_rest, 1)
                    pool.wait_ge(v_mid, n + 1)
                    wait(pool, d_pt, 48 * n)
                    pool.tensor_tensor(part[2][:, :, :], rest[:, :, :], part[1][:, :, :],
                                       ALU.subtract).then_inc(p_lo, 1)

                pool.memset(lnxb[:, :, 0:1], 0.0).then_inc(g_ones, 1)
                pool.wait_ge(g_ones, 1)
                pool.memset(ks[0][ST:ROWS, :, :], 1.0).then_inc(g_ones, 1)
                for k in range(2):
                    pool.wait_ge(g_ones, 2 + k)
                    pool.memset(kaug[k][:, :, :, HD:2 * HD], 1.0).then_inc(g_ones, 1)
                pool.wait_ge(g_ones, 4)
                for n in range(2):
                    norm(n)
                    split(n)
                for k in range(4):
                    pool.wait_ge(d_lnx[k], 64)
                pool.wait_ge(p_lo, 2)
                pool.memset(ks[1][ST:ROWS, :, :], 1.0).then_inc(g_ones, 1)
                pool.wait_ge(g_ones, 5)
                norm(2)
                split(2)
                with pool.Fori(3, B) as n:
                    norm(n)
                    split(n)

            @block.scalar
            def _(act):
                def h0_copy(n, i):
                    act.wait_ge(t_h0, 2 * n + i + 1)
                    if i == 0:
                        wait(act, v_z, NT * n)
                        wait(act, d_h0, 16 * n)
                    act.copy(h0[:, 2 * i:2 * i + 2, :],
                             mb[:, 0:2 * D].rearrange("p (t e) -> p t e", t=2)).then_inc(a_h0, 1)

                def zT_copy(n, c):
                    act.wait_ge(t_zt, 2 * n + c + 1)
                    wait(act, t_pr, 4 * n)
                    act.copy(zT[:, c, :], mb[0:C, :]).then_inc(a_zt, 1)

                def x_copy(n, c):
                    act.wait_ge(t_pr, 4 * n + c + 1)
                    if c == 0:
                        wait(act, p_rest, n)
                        wait(act, t_kt, 2 * n)
                    act.copy(x[:, c, :], mb[0:C, :]).then_inc(a_x, 1)

                def k_copy(n, par, c):
                    act.wait_ge(t_kt, 2 * n + c + 1)
                    wait(act, t_pv, 6 * (n - 1))
                    act.copy(kaug[par][:, :, 6 * c:6 * c + 6, 0:HD],
                             mb[:, 0:NT * C].rearrange("p (t h d) -> p t h d", t=NT, h=6)).then_inc(a_kt, 1)

                def y_copy(n, i):
                    act.wait_ge(t_op, 2 * n + i + 1)
                    wait(act, d_y, 16 * n)
                    act.copy(y[:, 2 * i:2 * i + 2, :],
                             mb[:, 0:2 * D].rearrange("p (t e) -> p t e", t=2)).then_inc(a_y, 1)

                def exp(b, s):
                    u = s // 4
                    act.wait_ge(t_qk, STEPS * b + s + 1)
                    if s % 4 == 0:
                        wait(act, t_pv, 6 * b + u - 1)
                    act.activation(E[:, u % 2, s % 4, :, :], ps[:, 2 * (s % 2):2 * (s % 2) + 2, :], ACT.Exp,
                                   scale=SCALE).then_inc(a_exp, 1)

                def sequence(b, par, first=False, front=True, last=False):
                    for s in range(STEPS):
                        exp(b, s)
                        if s in (3, 4) and front:
                            h0_copy(b + 2, s - 3)
                        if s in (5, 6) and not first:
                            y_copy(b - 1, s - 5)
                        if s in (7, 8) and not last:
                            k_copy(b + 1, 1 - par, s - 7)
                        if s in (10, 11) and front:
                            zT_copy(b + 2, s - 10)
                        if s in (12, 13, 14, 15) and front:
                            x_copy(b + 2, s - 12)

                act.wait_ge(g_ones, 4)
                for n in range(2):
                    for i in range(2):
                        h0_copy(n, i)
                    for c in range(2):
                        zT_copy(n, c)
                    for c in range(4):
                        x_copy(n, c)
                    if n == 0:
                        for c in range(2):
                            k_copy(0, 0, c)
                for k in range(4):
                    act.wait_ge(d_lnx[k], 64)
                sequence(0, 0, first=True)
                sequence(1, 1)
                with act.Fori(1, B // 2 - 1) as it:
                    sequence(2 * it, 0)
                    sequence(2 * it + 1, 1)
                sequence(B - 2, 0, front=False)
                sequence(B - 1, 1, front=False, last=True)
                for i in range(2):
                    y_copy(B - 1, i)

            @block.vector
            def _(dve):
                def norm(n):
                    dve.wait_ge(a_h0, 2 * n + 2)
                    for t in range(NT):
                        dve.bn_stats(st2[:, t, :], h0[:, t, :]).then_inc(v_s2, 1)
                    wait_apart(dve, v_s2, NT * n + NT, passed)
                    for t in range(NT):
                        dve.bn_aggr(mv2[:, t, :], st2[:, t, :]).then_inc(v_a2, 1)
                    dve.wait_ge(v_a2, NT * n + NT)
                    dve.tensor_scalar(ve2[:, :], mv2[:, :, 1], EPS, None, ALU.add).then_inc(v_v2, 1)

                def normalise(n):
                    dve.wait_ge(p_r2, n + 1)
                    wait(dve, t_zt, 2 * n)
                    for t in range(NT):
                        dve.tensor_scalar(z[:, t, :], h0[:, t, :], mv2[:, t, 0:1], rstd2[:, t:t + 1],
                                          ALU.subtract, ALU.mult).then_inc(v_z, 1)

                def high(n):
                    dve.wait_ge(a_x, 4 * n + 4)
                    wait(dve, d_pt, 48 * n)
                    dve.tensor_copy(part[0][:, :, :], x[:, :, :]).then_inc(v_hi, 1)

                def middle(n):
                    dve.wait_ge(p_rest, n + 1)
                    dve.tensor_copy(part[1][:, :, :], rest[:, :, :]).then_inc(v_mid, 1)

                def maxima(n, k):
                    dve.wait_ge(t_mx, STEPS * n + k + 1)
                    if k == 0:
                        wait(dve, t_mt, n)
                    dve.tensor_reduce(mx[:, 2 * (k % 2):2 * (k % 2) + 2, k // 2], ps[:, 4:6, :], AX_X,
                                      ALU.max).then_inc(v_mx, 1)

                def max_rows(n):
                    dve.wait_ge(t_mt, n + 1)
                    wait(dve, d_m, 32 * n)
                    dve.tensor_scalar(mrow[:, 0, :], mb[0:NH, :], -1.0, None, ALU.mult).then_inc(v_mh, 1)
                    dve.wait_ge(v_mh, n + 1)
                    dve.scalar_tensor_tensor(out=mrow[:, 1, :], in0=mb[0:NH, :], scalar=-1.0, in1=mrow[:, 0, :],
                                             op0=ALU.mult, op1=ALU.subtract).then_inc(v_m, 1)

                def weigh(n, g):
                    wait_apart(dve, t_pv, 6 * n + 2 * g + 2, passed)
                    dve.stream_shuffle(sums[:, :], ps[:, 6, :], [HD + r % HD for r in range(32)]).then_inc(v_sh, 1)
                    dve.wait_ge(v_sh, 3 * n + g + 1)
                    dve.reciprocal(recip[:, :], sums[:, :]).then_inc(v_rc, 1)
                    dve.wait_ge(v_rc, 3 * n + g + 1)
                    wait(dve, t_op, 2 * n)
                    dve.tensor_tensor(oT[:, g, :], ps[:, 6, :], recip[:, :], ALU.mult).then_inc(v_nm, 1)

                def sequence(b, par, first=False, front=True, last=False):
                    k = 0
                    for s in range(STEPS):
                        for _ in range(PAIRS_AT.count(s)):
                            if not last:
                                maxima(b + 1, k)
                                k += 1
                        if s == 2 and not first:
                            weigh(b - 1, 2)
                        if s == 5 and front:
                            norm(b + 2)
                        if s == 6 and front:
                            normalise(b + 2)
                        if s == 11:
                            weigh(b, 0)
                        if s == 16 and front:
                            high(b + 2)
                        if s == 19 and front:
                            middle(b + 2)
                        if s == 19:
                            weigh(b, 1)
                        if s == 22 and not last:
                            max_rows(b + 1)

                for n in range(2):
                    norm(n)
                    normalise(n)
                    high(n)
                    middle(n)
                for k in range(STEPS):
                    maxima(0, k)
                max_rows(0)
                sequence(0, 0, first=True)
                sequence(1, 1)
                with dve.Fori(1, B // 2 - 1) as it:
                    sequence(2 * it, 0)
                    sequence(2 * it + 1, 1)
                sequence(B - 2, 0, front=False)
                sequence(B - 1, 1, front=False, last=True)
                weigh(B - 1, 2)

            @block.tensor
            def _(pe):
                def h0_tiles(n, i):
                    if i == 0:
                        pe.wait_ge(d_x, 16 * n + 16)
                    else:
                        pe.wait_ge(a_h0, 2 * n + 1)
                    for t in range(2):
                        for c in range(2):
                            last = pe.matmul(mb[:, t * D:(t + 1) * D], lnxb[:, c, (2 * i + t) * P:(2 * i + t + 1) * P],
                                             M[:, c, :], start=(c == 0), stop=(c == 1))
                    last.then_inc(t_h0, 1)

                def z_transpose(n, c):
                    if c == 0:
                        pe.wait_ge(v_z, NT * n + NT)
                    else:
                        pe.wait_ge(a_zt, 2 * n + 1)
                    for t in range(NT):
                        last = pe.transpose(mb[0:C, t * P:(t + 1) * P], z[:, t, c * C:(c + 1) * C], ident[:, :])
                    last.then_inc(t_zt, 1)

                def project(n, c):
                    if c == 0:
                        pe.wait_ge(a_zt, 2 * n + 2)
                    else:
                        pe.wait_ge(a_x, 4 * n + c)
                    for k in range(2):
                        last = pe.matmul(mb[0:C, :], wqk_s[:, k, c * C:(c + 1) * C], zT[:, k, :],
                                         start=(k == 0), stop=(k == 1))
                    last.then_inc(t_pr, 1)

                def k_transpose(n, c):
                    if c == 0:
                        pe.wait_ge(a_x, 4 * n + 4)
                    else:
                        pe.wait_ge(a_kt, 2 * n + 1)
                    for t in range(NT):
                        last = pe.transpose(mb[:, t * C:(t + 1) * C], x[:, 2 + c, t * P:(t + 1) * P], ident[0:C, 0:C])
                    last.then_inc(t_kt, 1)

                def max_scores(n, par, k):
                    h = k // 2
                    if k % 8 == 0:
                        pe.wait_ge(d_st[h // 4], 192 * n + 192)
                    wait(pe, v_mx, STEPS * n + k)
                    for i in range(2):
                        t = 2 * (k % 2) + i
                        last = pe.matmul(ps[:, 4 + i, :], qs[par][0:ST, h, t * P:(t + 1) * P], ks[par][0:ST, h, :],
                                         start=True, stop=True)
                    last.then_inc(t_mx, 1)

                def max_transpose(n):
                    pe.wait_ge(v_mx, STEPS * n + STEPS)
                    for t in range(NT):
                        last = pe.transpose(mb[0:NH, t * P:(t + 1) * P], mx[:, t, :], ident[:, :])
                    last.then_inc(t_mt, 1)

                def scores(b, par, s):
                    h = 4 * (s // 8) + s % 4
                    if s == 0:
                        pe.wait_ge(d_m, 32 * b + 32)
                    wait(pe, a_exp, STEPS * b + s - 1)
                    for i in range(2):
                        t = 2 * (s // 4 % 2) + i
                        last = pe.matmul(ps[:, 2 * (s % 2) + i, :], ks[par][0:ROWS, h, t * P:(t + 1) * P],
                                         qs[par][0:ROWS, h, :], start=True, stop=True)
                    last.then_inc(t_qk, 1)

                def values(b, par, u):
                    if u == 0:
                        pe.wait_ge(a_kt, 2 * b + 2)
                    if u % 2 == 0:
                        wait(pe, v_nm, 3 * b + u // 2)
                    pe.wait_ge(a_exp, STEPS * b + 4 * u + 4)
                    for i in range(2):
                        t = 2 * (u % 2) + i
                        for j in range(4):
                            last = pe.matmul(ps[32 * j:32 * j + 32, 6, :], kaug[par][:, t, 4 * (u // 2) + j, :],
                                             E[:, u % 2, j, i, :], start=(t == 0), stop=(t == NT - 1))
                    last.then_inc(t_pv, 1)

                def out_tiles(n, i):
                    if i == 0:
                        pe.wait_ge(v_nm, 3 * n + 3)
                    else:
                        pe.wait_ge(a_y, 2 * n + 1)
                    for t in range(2):
                        for g in range(3):
                            last = pe.matmul(mb[:, t * D:(t + 1) * D], oT[:, g, (2 * i + t) * P:(2 * i + t + 1) * P],
                                             wout_s[:, g, :], start=(g == 0), stop=(g == 2))
                    last.then_inc(t_op, 1)

                def sequence(b, par, first=False, front=True, last=False):
                    k = 0
                    for s in range(STEPS):
                        scores(b, par, s)
                        for _ in range(PAIRS_AT.count(s)):
                            if not last:
                                max_scores(b + 1, 1 - par, k)
                                k += 1
                        if s == 1 and not first:
                            values(b - 1, 1 - par, 5)
                        if s in (3, 4) and front:
                            pe.wait_ge(v_m, b + 1)
                            h0_tiles(b + 2, s - 3)
                        if s in (5, 6) and not first:
                            if front:
                                pe.wait_ge(a_h0, 2 * (b + 2) + 2)
                            else:
                                pe.wait_ge(v_m, b + 1)
                            out_tiles(b - 1, s - 5)
                        if s in (7, 8) and not last:
                            if front:
                                pe.wait_ge(a_h0, 2 * (b + 2) + 2)
                            wait(pe, a_y, 2 * b)
                            k_transpose(b + 1, s - 7)
                        if s in (6, 10, 14, 18, 22):
                            values(b, par, s // 4 - 1)
                        if s in (10, 11) and front:
                            pe.wait_ge(a_kt, 2 * (b + 1) + 2)
                            z_transpose(b + 2, s - 10)
                        if s in (12, 13, 14, 15) and front:
                            project(b + 2, s - 12)
                        if s == 22 and not last:
                            if front:
                                pe.wait_ge(a_x, 4 * (b + 2) + 4)
                            pe.wait_ge(a_kt, 2 * (b + 1) + 2)
                            max_transpose(b + 1)

                pe.wait_ge(g_ones, 4)
                for n in range(2):
                    if n:
                        pe.wait_ge(a_kt, 2)
                    for i in range(2):
                        h0_tiles(n, i)
                    for c in range(2):
                        z_transpose(n, c)
                    for c in range(4):
                        project(n, c)
                    if n == 0:
                        for c in range(2):
                            k_transpose(0, c)
                for k in range(STEPS):
                    max_scores(0, 0, k)
                pe.wait_ge(a_x, 8)
                max_transpose(0)
                pe.wait_ge(g_ones, 5)
                sequence(0, 0, first=True)
                sequence(1, 1)
                with pe.Fori(1, B // 2 - 1) as it:
                    sequence(2 * it, 0)
                    sequence(2 * it + 1, 1)
                sequence(B - 2, 0, front=False)
                sequence(B - 1, 1, front=False, last=True)
                values(B - 1, 1, 5)
                for i in range(2):
                    out_tiles(B - 1, i)

        with ExitStack() as ph:
            hin = [sb(f"hin{k}", [P, NT, D], F32, ph) for k in range(2)]
            yin = [sb(f"yin{k}", [P, NT, D], F32, ph) for k in range(2)]
            hb = [sb(f"hb{k}", [P, NT, D], F32, ph) for k in range(2)]
            fz = sb("fz", [P, NT, D], F32, ph)
            st3 = sb("st3", [P, NT, 6], F32, ph)
            mv3 = sb("mv3", [P, NT, 2], F32, ph)
            ve3 = sb("ve3", [P, NT], F32, ph)
            rstd3 = sb("rstd3", [P, NT], F32, ph)
            fzT = [sb(f"fzT{k}", [C, 2, S], F32, ph) for k in range(2)]
            act_s = [sb(f"act{k}", [P, HC, S], F32, ph) for k in range(2)]
            res = [sb(f"res{k}", [P, NT, D], F32, ph) for k in range(2)]

            f_ld = [sem(f"f_ld{k}") for k in range(2)]
            f_out = [sem(f"f_out{k}") for k in range(2)]
            f_h = sem("f_h")
            f_st, f_ag, f_var, f_rstd = sem("f_st"), sem("f_ag"), sem("f_var"), sem("f_rstd")
            f_z = sem("f_z")
            f_hb = sem("f_hb")
            f_zt, f_zc = sem("f_zt"), sem("f_zc")
            f_up, f_act = sem("f_up"), sem("f_act")
            f_dn, f_res = sem("f_dn"), sem("f_res")

            block = ph.enter_context(nc.Block())

            @block.sync
            def _(sp):
                def load(n, k):
                    wait(sp, f_res, 2 * (n - 1))
                    for to, of in ((hin[k], h0_d), (yin[k], y_d)):
                        sp.dma_start(to[:, :, :].rearrange("p t e -> p (t e)"),
                                     of[bass.ds(n, 1), :, :].rearrange("o p m -> (o p) m")).then_inc(f_ld[k], 16)

                def store(n, k):
                    wait_apart(sp, f_res, 2 * n + 2, passed)
                    sp.dma_start(out[bass.ds(n, 1), :, :].rearrange("o (t p) e -> p (o t) e", p=P),
                                 res[k][:, :, :]).then_inc(f_out[k], 16)

                load(0, 0)
                load(1, 1)
                with sp.Fori(0, B // 2 - 1) as it:
                    for k in range(2):
                        store(2 * it + k, k)
                        load(2 * it + k + 2, k)
                for k in range(2):
                    store(B - 2 + k, k)
                for k in range(2):
                    sp.wait_ge(f_out[k], 16 * (B // 2))

            @block.gpsimd
            def _(pool):
                with pool.Fori(0, B // 2) as it:
                    for k in range(2):
                        n = 2 * it + k
                        pool.wait_ge(f_var, n + 1)
                        pool.tensor_tensor(rstd3[:, :], ve3[:, :], half[:, :], ALU.pow).then_inc(f_rstd, 1)
                        for t in range(NT):
                            pool.tensor_tensor(hb[k][:, t, :], hin[k][:, t, :], b1[:, :], ALU.add).then_inc(f_hb, 1)

            @block.scalar
            def _(act):
                def z_copy(n, k, c):
                    act.wait_ge(f_zt, 2 * n + c + 1)
                    act.copy(fzT[k][:, c, :], ps[0:C, 4 + c, :]).then_inc(f_zc, 1)

                def gelu(n, k, m):
                    act.wait_ge(f_up, HC * n + m + 1)
                    if m == 0:
                        wait(act, f_dn, 2 * (n - 1))
                    act.activation(act_s[k][:, m, :], ps[:, (2 * k + m) % 4, :], ACT.Gelu_apprx_tanh,
                                   bias=b0[:, m:m + 1]).then_inc(f_act, 1)

                def sequence(n, k, last=False):
                    for m in range(HC):
                        gelu(n, k, m)
                        if m in (3, 4) and not last:
                            z_copy(n + 1, 1 - k, m - 3)

                for c in range(2):
                    z_copy(0, 0, c)
                sequence(0, 0)
                sequence(1, 1)
                with act.Fori(1, B // 2 - 1) as it:
                    sequence(2 * it, 0)
                    sequence(2 * it + 1, 1)
                sequence(B - 2, 0)
                sequence(B - 1, 1, last=True)

            @block.vector
            def _(dve):
                def norm(n, k):
                    dve.wait_ge(f_ld[k], 16 * (n - k) + 32)
                    dve.tensor_tensor(hin[k][:, :, :], hin[k][:, :, :], yin[k][:, :, :], ALU.add).then_inc(f_h, 1)
                    dve.wait_ge(f_h, n + 1)
                    for t in range(NT):
                        dve.bn_stats(st3[:, t, :], hin[k][:, t, :]).then_inc(f_st, 1)
                    wait_apart(dve, f_st, NT * n + NT, passed)
                    for t in range(NT):
                        dve.bn_aggr(mv3[:, t, :], st3[:, t, :]).then_inc(f_ag, 1)
                    dve.wait_ge(f_ag, NT * n + NT)
                    dve.tensor_scalar(ve3[:, :], mv3[:, :, 1], EPS, None, ALU.add).then_inc(f_var, 1)
                    dve.wait_ge(f_rstd, n + 1)
                    wait(dve, f_zt, 2 * n)
                    for t in range(NT):
                        dve.tensor_scalar(fz[:, t, :], hin[k][:, t, :], mv3[:, t, 0:1], rstd3[:, t:t + 1],
                                          ALU.subtract, ALU.mult).then_inc(f_z, 1)

                def result(n, k, i):
                    dve.wait_ge(f_dn, 2 * n + i + 1)
                    if i == 0:
                        dve.wait_ge(f_hb, NT * n + NT)
                        wait(dve, f_out[k], 8 * (n - k))
                    dve.tensor_tensor(res[k][:, 2 * i:2 * i + 2, :],
                                      ps[:, 6 + i, 0:2 * D].rearrange("p (t e) -> p t e", t=2),
                                      hb[k][:, 2 * i:2 * i + 2, :], ALU.add).then_inc(f_res, 1)

                norm(0, 0)
                norm(1, 1)
                for k in range(2):
                    for i in range(2):
                        result(k, k, i)
                    norm(2 + k, k)
                with dve.Fori(1, B // 2 - 1) as it:
                    for k in range(2):
                        for i in range(2):
                            result(2 * it + k, k, i)
                        norm(2 * it + k + 2, k)
                for k in range(2):
                    for i in range(2):
                        result(B - 2 + k, k, i)

            @block.tensor
            def _(pe):
                def z_transpose(n, k, c):
                    pe.wait_ge(f_z, NT * n + NT)
                    wait(pe, f_zc, 2 * n)
                    for t in range(NT):
                        last = pe.transpose(ps[0:C, 4 + c, t * P:(t + 1) * P], fz[:, t, c * C:(c + 1) * C], ident[:, :])
                    last.then_inc(f_zt, 1)

                def up(n, k, m):
                    if m == 0:
                        pe.wait_ge(f_zc, 2 * n + 2)
                    wait(pe, f_act, HC * n + m - 3)
                    for c in range(2):
                        last = pe.matmul(ps[:, (2 * k + m) % 4, :], w0[:, c, m * P:(m + 1) * P], fzT[k][:, c, :],
                                         start=(c == 0), stop=(c == 1))
                    last.then_inc(f_up, 1)

                def down(n, k, i):
                    wait(pe, f_res, 2 * (n - 1) + i + 1)
                    for t in range(2):
                        for m in range(HC):
                            if i == 0 and t == 0:
                                pe.wait_ge(f_act, HC * n + m + 1)
                            last = pe.matmul(ps[:, 6 + i, t * D:(t + 1) * D],
                                             act_s[k][:, m, (2 * i + t) * P:(2 * i + t + 1) * P], w1[:, m, :],
                                             start=(m == 0), stop=(m == HC - 1))
                    last.then_inc(f_dn, 1)

                def sequence(n, k, last=False):
                    for m in range(HC):
                        up(n, k, m)
                        if m in (3, 4) and not last:
                            z_transpose(n + 1, 1 - k, m - 3)
                    for i in range(2):
                        down(n, k, i)

                for c in range(2):
                    z_transpose(0, 0, c)
                sequence(0, 0)
                sequence(1, 1)
                with pe.Fori(1, B // 2 - 1) as it:
                    sequence(2 * it, 0)
                    sequence(2 * it + 1, 1)
                sequence(B - 2, 0)
                sequence(B - 1, 1, last=True)


def layouts(x, wte, W_proj, ln_w, ln_b, W_val, W_out, trace0, w_qkv, w_out, w_fc, b_fc, w_proj, b_proj, ae, ar):
    chunks = lambda w: np.ascontiguousarray(w.reshape(2, C, -1).transpose(1, 0, 2))
    pieces = x.reshape(B * CH, TS)
    ids = np.concatenate([pieces, np.roll(pieces, -1, axis=0)[:, :LAG]], axis=1)
    return {
        "ids": np.ascontiguousarray(ids), "wte": wte,
        "wpT": chunks(W_proj.T), "wvT": chunks(W_val.T),
        "wpN": np.ascontiguousarray(W_proj.reshape(TH, TD, D).transpose(1, 0, 2)),
        "woT": np.ascontiguousarray(W_out.T.reshape(TH, TD, D).transpose(1, 0, 2)),
        "t0T": np.ascontiguousarray(trace0.transpose(2, 0, 1)),
        "lnw": np.ascontiguousarray(ln_w.reshape(2, C).T), "lnb": np.ascontiguousarray(ln_b.reshape(2, C).T),
        "wqk": chunks(w_qkv[:, :2 * D]), "wout": w_out,
        "w0T": chunks(w_fc.T), "bfc": np.ascontiguousarray(b_fc.reshape(HC, P).T),
        "w1T": np.ascontiguousarray(w_proj.T.reshape(HC, P, D).transpose(1, 0, 2)), "bproj": b_proj.reshape(1, D),
        "al_e": ae.reshape(1, 3), "al_r": ar.reshape(1, 3),
    }


_INS = ['x', 'L0_tok_wte', 'L0_tok_W_proj', 'L0_tok_ln_w', 'L0_tok_ln_b', 'L0_tok_W_val', 'L0_tok_W_out',
        'L0_tok_trace0', 'L0_attn_w_qkv', 'L0_attn_w_out', 'L0_ffn_w_fc', 'L0_ffn_b_fc', 'L0_ffn_w_proj',
        'L0_ffn_b_proj', 'L0_ffn_alpha_e', 'L0_ffn_alpha_r']


def kernel(**inputs):
    import concourse.bacc as bacc
    from concourse.bass_utils import run_bass_kernel_spmd

    arrays = layouts(*(np.asarray(inputs[name]) for name in _INS))
    nc = bacc.Bacc("TRN2", target_bir_lowering=False, num_devices=1)
    ins = {k: nc.dram_tensor(k, v.shape, mybir.dt.from_np(v.dtype), kind="ExternalInput").ap()
           for k, v in arrays.items()}
    out = nc.dram_tensor("out", (B, S, D), F32, kind="ExternalOutput").ap()
    tower(nc, *ins.values(), out)
    r = run_bass_kernel_spmd(nc, [arrays], core_ids=[0])
    return r.results[0]["out"]
```

```python
from contextlib import ExitStack

import numpy as np
import concourse.bass as bass
from concourse import mybir

F32 = mybir.dt.float32
BF16 = mybir.dt.bfloat16
I32 = mybir.dt.int32
ACT = mybir.ActivationFunctionType
ALU = mybir.AluOpType
AX_X = mybir.AxisListType.X

P = 128
B, S, D = 16, 512, 192
C = D // 2
CH = 8
TS = S // CH
LAG = 2
NG = TS // 4
TH, TD = 8, 64
NH, HD = 12, 16
NT = S // P
HID, HC = 768, 6
EPS = 1e-5
DECAY = 0.99
UPDATE = 0.1 / (B * (S - LAG))
SCALE = float(D) ** -0.5
EMBED = [96, 144, 192]
RATIO = [2, 3, 4]
QPARTS = [0, 0, 1, 0, 1, 2]
KPARTS = [0, 1, 0, 2, 1, 0]
ST = 6 * HD
MAXIMA = NH * NT
STEPS = 24
LATE_MAX_AT = 0
H0_AT = (1, 2)
KEYS_AT = (3, 4)
LAST_SUMS_AT = 5
NORM_AT = (7, 8)
PROJECT_AT = (9, 10, 11, 12)
HEADS_AT = (13, 14)
SUMS_AT = (15, 20)
OUT_AT = (16, 17)
EARLY_MAX_AT = 18
VALUES_AT = (6, 10, 14, 18, 22)
LAST_VALUES_AT = 1
MAX_AT = [(1, 0, 0, 0, 0)] * STEPS
for _s in (1, 10):
    MAX_AT[_s] = (1, 1, 1, 1, 0)
for _s in (6, 14, 18, 22):
    MAX_AT[_s] = (1, 1, 0, 0, 1)
for _s in (2, 9, 11, 12):
    MAX_AT[_s] = (1, 0, 0, 1, 1)
for _s in OUT_AT:
    MAX_AT[_s] = (1, 0, 0, 1, 0)
MAX_ALONE = [(0, 0, 0, 0, 12) if 13 <= s < 17 else (0, 0, 0, 0, 0) for s in range(STEPS)]
LOTS = [(0, 8), (8, NH)]


def wait(eng, sem, value):
    if not (isinstance(value, int) and value <= 0):
        eng.wait_ge(sem, value)


def wait_apart(eng, sem, value, passed):
    wait(eng, sem, value)
    if not isinstance(value, int):
        eng.sem_inc(passed, 1)


def tower(nc, ids, wte, wpT, wvT, wpN, woT, t0T, lnw, lnb, wqk, wout, w0T, bfc, w1T, bproj,
          al_e, al_r, out):
    lnx_d = nc.dram_tensor("lnx_d", [B, C, 2, S], F32).ap()
    parts_d = nc.dram_tensor("parts_d", [3, 4 * C, S], BF16).ap()
    h0_d = nc.dram_tensor("h0_d", [B, P, NT * D], F32).ap()
    y_d = nc.dram_tensor("y_d", [B, P, NT * D], F32).ap()

    with ExitStack() as top:
        def sb(name, shape, dt, ctx=top):
            return ctx.enter_context(nc.sbuf_tensor(name, shape, dt))

        def sem(name):
            return top.enter_context(nc.semaphore(name))

        ps = top.enter_context(nc.psum_tensor("ps", [P, 8, 512], F32))
        ident = sb("ident", [P, P], F32)
        M = sb("M", [C, 2, D], F32)
        w0 = sb("w0", [C, 2, HID], F32)
        w1 = sb("w1", [P, HC, D], F32)
        b0 = sb("b0", [P, HC], F32)
        b1 = sb("b1", [P, D], F32)
        wqk_s = sb("wqk_s", [C, 2, 2 * D], F32)
        wout_s = sb("wout_s", [C, 2, D], F32)
        half = sb("half", [P, 4], F32)
        wide = sb("wide", [P, 2 * B * S], F32)

        passed = sem("passed")
        d_const = sem("d_const")
        d_ffn = sem("d_ffn")
        g_const = sem("g_const")
        d_lnx = [sem(f"d_lnx{k}") for k in range(4)]

        with ExitStack() as ph:
            tok = sb("tok", [P, TS + LAG, D], F32, ph)
            xn = sb("xn", [P, 2, 4, D + 2], F32, ph)
            idx = sb("idx", [P, TS + LAG], I32, ph)
            keeps = sb("keeps", [P, B], F32, ph)
            keep = sb("keep", [P, 1], F32, ph)
            st = sb("st", [P, 4, 6], F32, ph)
            mv = sb("mv", [P, 4, 2], F32, ph)
            ve = sb("ve", [P, 4], F32, ph)
            rstd = sb("rstd", [P, 4], F32, ph)
            zero = sb("zero", [P, D], F32, ph)
            wp = sb("wp", [C + 1, 2, TH * TD], F32, ph)
            wv = sb("wv", [C, 2, TH * TD], F32, ph)
            wpn = sb("wpn", [TD, TH, D], F32, ph)
            wo = sb("wo", [TD, TH, D], F32, ph)
            t0 = sb("t0", [TD, TH, TD], F32, ph)
            lw = sb("lw", [C, 2], F32, ph)
            lb = sb("lb", [C, 2], F32, ph)
            bcol = sb("bcol", [C, 2, C + 1], F32, ph)
            G = sb("G", [C + 1, 2, D], F32, ph)
            U = sb("U", [C, 2, TH * TD], F32, ph)
            trace = sb("trace", [TD, TH, TD], F32, ph)
            X = sb("X", [TD, TH, D], F32, ph)

            gath = [sem(f"gath{k}") for k in range(4)]
            gath_tail = sem("gath_tail")
            d_idx = sem("d_idx")
            v_st = sem("v_st")
            v_ag = sem("v_ag")
            v_var = sem("v_var")
            p_rstd = sem("p_rstd")
            v_xn = sem("v_xn")
            t_tr = sem("t_tr")
            a_ln = sem("a_ln")
            t_G = sem("t_G")
            v_ch = sem("v_ch")
            v_bcol = sem("v_bcol")
            t_bw = sem("t_bw")
            v_wp = sem("v_wp")
            t_m = sem("t_m")
            c_m = sem("c_m")

            lnx = wide[0:C, :].rearrange("p (c n) -> p c n", c=2)
            tr = [[ps[0:C, 2 * k + c, :].rearrange("p (t q) -> p t q", t=4) for c in range(2)] for k in range(2)]
            G_ps = [ps[0:C, 4, 0:D], ps[0:C + 1, 5, 0:D]]
            trace_ps = ps[0:TD, 6, :].rearrange("p (h q) -> p h q", h=TH)
            X_ps = ps[0:TD, 0:4, 0:2 * D]
            M_ps = ps[0:C, 4:6, 0:D]

            def tile_of(t):
                return tok[:, bass.ds(t, 1), :].rearrange("p o f -> p (o f)")

            block = ph.enter_context(nc.Block())

            @block.sync
            def _(sp):
                sp.dma_start(idx[:, :], ids).then_inc(d_idx, 16)
                for to, of in ((lw[:, :], lnw), (lb[:, :], lnb), (wp[0:C, :, :], wpT), (wv[:, :, :], wvT),
                               (wpn[:, :, :], wpN), (wo[:, :, :], woT), (t0[:, :, :], t0T), (wqk_s[:, :, :], wqk),
                               (wout_s[:, :, :], wout)):
                    sp.dma_start(to, of).then_inc(d_const, 16)
                for to, of in ((w0[:, :, :], w0T), (w1[:, :, :], w1T), (b0[:, :], bfc),
                               (b1[:, :], bproj.to_broadcast([P, D]))):
                    sp.dma_start(to, of).then_inc(d_ffn, 16)
                sp.wait_ge(a_ln, 2 * NG)
                for b in range(B):
                    sp.dma_start(lnx_d[b, :, :, :], lnx[:, :, b * S:(b + 1) * S]).then_inc(d_lnx[b // 4], 16)

            @block.gpsimd
            def _(pool):
                pool.wait_ge(d_idx, 16)

                def gather(t, done):
                    pool.indirect_dma_start(out=tok[:, t, :], out_offset=None, in_=wte,
                                            in_offset=bass.IndirectOffsetOnAxis(ap=idx[:, t:t + 1], axis=0)
                                            ).then_inc(done, 16)

                for t in range(12):
                    gather(t, gath[t // 4])
                pool.memset(half[:, :], -0.5).then_inc(g_const, 1)
                pool.memset(ident[:, :], 0.0).then_inc(g_const, 1)
                pool.memset(keeps[:, :], 1.0).then_inc(g_const, 1)
                pool.wait_ge(g_const, 3)
                pool.affine_select(out=ident[:, :], in_=ident[:, :], compare_op=ALU.not_equal, fill=1.0,
                                   base=0, pattern=[[-1, P]], channel_multiplier=1).then_inc(g_const, 1)
                pool.affine_select(out=keeps[:, :], in_=keeps[:, :], compare_op=ALU.not_equal, fill=0.0,
                                   base=-(CH - 1), pattern=[[-CH, B]], channel_multiplier=1).then_inc(g_const, 1)
                for g in range(NG):
                    if g + 3 < NG:
                        if g + 3 >= 4:
                            pool.wait_ge(gath[(g + 3) % 4], 64 * ((g + 3) // 4))
                        for t in range(4 * (g + 3), 4 * (g + 4)):
                            gather(t, gath[(g + 3) % 4])
                    if g == NG - 4:
                        for t in range(TS, TS + LAG):
                            gather(t, gath_tail)
                    pool.wait_ge(v_var, g + 1)
                    pool.tensor_tensor(rstd[:, :], ve[:, :], half[:, :], ALU.pow).then_inc(p_rstd, 1)

            @block.scalar
            def _(act):
                act.wait_ge(d_const, 16 * 9)
                with act.Fori(0, NG // 2) as it:
                    for k in range(2):
                        g = 2 * it + k
                        act.wait_ge(t_tr, g + 1)
                        for c in range(2):
                            view = lnx[:, c, :].rearrange("p (q t) -> p t q", t=TS)
                            act.activation(view[:, bass.ds(4 * g, 4), :], tr[k][c], ACT.Identity,
                                           scale=lw[:, c:c + 1], bias=lb[:, c:c + 1]).then_inc(a_ln, 1)
                act.wait_ge(t_m, 1)
                for i in range(2):
                    act.copy(G[0:C + i, i, :], G_ps[i]).then_inc(c_m, 1)
                act.wait_ge(t_m, 2)
                for i in range(2):
                    act.copy(U[:, i, :], ps[0:C, i, :]).then_inc(c_m, 1)
                act.wait_ge(t_m, 4)
                act.copy(X[:, :, :].rearrange("p (i h) e -> p i (h e)", h=2), X_ps).then_inc(c_m, 1)
                act.wait_ge(t_m, 5)
                act.copy(M[:, :, :], M_ps).then_inc(c_m, 1)

            @block.vector
            def _(dve):
                dve.memset(xn[:, :, :, D:D + 1], 1.0).then_inc(v_ch, 1)
                dve.memset(zero[:, :], 0.0).then_inc(v_ch, 1)
                dve.memset(bcol[:, :, :], 0.0).then_inc(v_ch, 1)
                dve.wait_ge(v_ch, 3)
                dve.wait_ge(d_const, 16 * 9)
                dve.tensor_copy(bcol[:, :, C:C + 1], lb[:, :].rearrange("p (c o) -> p c o", o=1)).then_inc(v_bcol, 1)
                dve.wait_ge(t_bw, 1)
                for c in range(2):
                    dve.tensor_scalar(wp[0:C, c, :], wp[0:C, c, :], lw[:, c:c + 1], None, ALU.mult).then_inc(v_wp, 1)
                dve.tensor_copy(wp[C:C + 1, 1, :], ps[C:C + 1, 6, :]).then_inc(v_wp, 1)
                dve.tensor_scalar(t0[:, :, :], t0[:, :, :], DECAY, None, ALU.mult).then_inc(v_wp, 1)

                with dve.Fori(0, NG // 4) as it:
                    for k in range(4):
                        g = 4 * it + k
                        dve.wait_ge(gath[k], 64 * (it + 1))
                        for j in range(4):
                            dve.bn_stats(st[:, j, :], tile_of(4 * g + j)).then_inc(v_st, 1)
                        wait_apart(dve, v_st, 4 * g + 4, passed)
                        for j in range(4):
                            dve.bn_aggr(mv[:, j, :], st[:, j, :]).then_inc(v_ag, 1)
                        dve.wait_ge(v_ag, 4 * g + 4)
                        dve.tensor_scalar(ve[:, :], mv[:, :, 1], EPS, None, ALU.add).then_inc(v_var, 1)
                        dve.wait_ge(t_G, g + 1)
                        dve.wait_ge(p_rstd, g + 1)
                        for j in range(4):
                            dve.tensor_scalar(xn[:, k % 2, j, 0:D], tile_of(4 * g + j), mv[:, j, 0:1],
                                              rstd[:, j:j + 1], ALU.subtract, ALU.mult).then_inc(v_xn, 1)

                dve.wait_ge(g_const, 5)
                dve.tensor_reduce(keep[:, :], keeps[:, :], AX_X, ALU.min).then_inc(v_ch, 1)
                dve.wait_ge(v_ch, 4)
                dve.wait_ge(gath_tail, 16 * LAG)
                dve.tensor_scalar(tok[:, TS:TS + LAG, :], tok[:, TS:TS + LAG, :], keep[:, 0:1], None,
                                  ALU.mult).then_inc(v_ag, 4)
                dve.wait_ge(t_m, 3)
                dve.scalar_tensor_tensor(out=trace[:, :, :], in0=trace_ps, scalar=UPDATE, in1=t0[:, :, :],
                                         op0=ALU.mult, op1=ALU.add).then_inc(c_m, 1)

            @block.tensor
            def _(pe):
                pe.wait_ge(v_bcol, 1)
                for c in range(2):
                    last = pe.matmul(ps[0:C + 1, 6, :], bcol[:, c, :], wp[0:C, c, :], start=(c == 0), stop=(c == 1))
                last.then_inc(t_bw, 1)
                pe.matmul(G_ps[0], zero[:, 0:C], zero[:, :], start=True, stop=False).then_inc(t_G, 1)
                pe.matmul(G_ps[1], zero[:, 0:C + 1], zero[:, :], start=True, stop=False).then_inc(t_G, 1)
                pe.wait_ge(g_const, 4)

                def group(g, k):
                    pe.wait_ge(v_xn, 4 * g + 4)
                    wait(pe, a_ln, 2 * (g - 1))
                    for c in range(2):
                        for j in range(4):
                            last = pe.transpose(tr[k][c][:, j, :], xn[:, k, j, c * C:(c + 1) * C], ident[:, :])
                    last.then_inc(t_tr, 1)
                    pe.wait_ge(v_ag, 4 * (g + 2))
                    for j in range(4):
                        later = tile_of(4 * g + j + LAG)
                        pe.matmul(G_ps[0], xn[:, k, j, 0:C], later, start=False, stop=False)
                        last = pe.matmul(G_ps[1], xn[:, k, j, C:D + 1], later, start=False, stop=False)
                    last.then_inc(t_G, 1)

                group(0, 0)
                group(1, 1)
                with pe.Fori(1, NG // 2) as it:
                    group(2 * it, 0)
                    group(2 * it + 1, 1)
                pe.matmul(G_ps[0], zero[:, 0:C], zero[:, :], start=False, stop=True)
                pe.matmul(G_ps[1], zero[:, 0:C + 1], zero[:, :], start=False, stop=True).then_inc(t_m, 1)
                pe.wait_ge(c_m, 2)
                pe.wait_ge(v_wp, 4)
                pe.wait_ge(a_ln, 2 * NG)
                for i in range(2):
                    for c in range(2):
                        last = pe.matmul(ps[0:C, i, :], G[0:C + c, c, i * C:(i + 1) * C], wp[0:C + c, c, :],
                                         start=(c == 0), stop=(c == 1))
                last.then_inc(t_m, 1)
                pe.wait_ge(c_m, 4)
                for h in range(TH):
                    for c in range(2):
                        last = pe.matmul(trace_ps[:, h, :], wv[:, c, h * TD:(h + 1) * TD],
                                         U[:, c, h * TD:(h + 1) * TD], start=(c == 0), stop=(c == 1))
                last.then_inc(t_m, 1)
                pe.wait_ge(c_m, 5)
                for h in range(TH):
                    last = pe.matmul(X_ps[:, h // 2, D * (h % 2):D * (h % 2) + D], trace[:, h, :], wo[:, h, :],
                                     start=True, stop=True)
                last.then_inc(t_m, 1)
                pe.wait_ge(c_m, 6)
                for i in range(2):
                    for h in range(TH):
                        last = pe.matmul(M_ps[:, i, :], wpn[:, h, i * C:(i + 1) * C], X[:, h, :],
                                         start=(h == 0), stop=(h == TH - 1))
                last.then_inc(t_m, 1)

        with ExitStack() as ph:
            lnxb = sb("lnxb", [C, 2, S], F32, ph)
            h0 = sb("h0", [P, NT, D], F32, ph)
            z = sb("z", [P, NT, D], F32, ph)
            st2 = sb("st2", [P, NT, 6], F32, ph)
            mv2 = sb("mv2", [P, NT, 2], F32, ph)
            ve2 = sb("ve2", [P, NT], F32, ph)
            rstd2 = sb("rstd2", [P, NT], F32, ph)
            zT = sb("zT", [C, 2, S], F32, ph)
            x = sb("x", [C, 4, S], F32, ph)
            rest = sb("rest", [C, 4, S], F32, ph)
            part = [sb(f"part{r}", [C, 4, S], BF16, ph) for r in range(3)]
            kaug = [sb(f"kaug{k}", [P, NT, NH, 2 * HD], F32, ph) for k in range(2)]
            mx = sb("mx", [P, NT, NH], F32, ph)
            mrow = [sb(f"mrow{k}", [hi - lo, 2, S], BF16, ph) for k, (lo, hi) in enumerate(LOTS)]
            o = sb("o", [P, S], F32, ph)
            recip = sb("recip", [P, NT, 4, 1], F32, ph)
            at = sb("at", [P, NT, D], F32, ph)
            aT = sb("aT", [C, 2, S], F32, ph)
            y = sb("y", [P, NT, D], F32, ph)
            ae = sb("ae", [P, 3], F32, ph)
            ar = sb("ar", [P, 3], F32, ph)
            a = sb("a", [P, 9], F32, ph)
            hm = sb("hm", [P, 9, HC], F32, ph)
            em = sb("em", [C, 1], F32, ph)
            hma = sb("hma", [P, 9, HC], F32, ph)
            ema = sb("ema", [C, 9], F32, ph)
            c0 = sb("c0", [C, 2, HID], F32, ph)
            c1 = sb("c1", [P, HC, D], F32, ph)
            c0b = sb("c0b", [P, HC], F32, ph)
            c1b = sb("c1b", [P, D], F32, ph)
            q_even = sb("q_even", [P, NH, S], BF16, ph)
            k_even = sb("k_even", [P, NH, S], BF16, ph)
            E = wide[:, 0:16 * S].rearrange("p (u j i n) -> p u j i n", u=2, j=4, i=2)
            odd = wide[:, 16 * S:16 * S + NH * S].bitcast(BF16).rearrange("p (a h n) -> p a h n", a=2, h=NH)
            qs = [q_even[:, :, :], odd[:, 0, :, :]]
            ks = [k_even[:, :, :], odd[:, 1, :, :]]
            ROWS = ST + 2

            g_ones = sem("g_ones")
            d_x = sem("d_x")
            d_h0 = sem("d_h0")
            d_pt = [sem(f"d_pt{r}") for r in range(3)]
            d_st = [sem(f"d_st{g}") for g in range(3)]
            d_m = [sem(f"d_m{k}") for k in range(2)]
            d_y = sem("d_y")
            t_h0, a_h0 = sem("t_h0"), sem("a_h0")
            v_s2, v_a2, v_v2, p_r2 = sem("v_s2"), sem("v_a2"), sem("v_v2"), sem("p_r2")
            v_z = sem("v_z")
            t_zt, a_zt = sem("t_zt"), sem("a_zt")
            t_pr, a_x = sem("t_pr"), sem("a_x")
            a_hi = sem("a_hi")
            p_rest, v_mid, p_lo = sem("p_rest"), sem("v_mid"), sem("p_lo")
            t_kt, a_kt = sem("t_kt"), sem("a_kt")
            t_mx, v_mx = sem("t_mx"), sem("v_mx")
            t_mt = sem("t_mt")
            v_mh, v_m = sem("v_mh"), sem("v_m")
            t_qk, a_exp = sem("t_qk"), sem("a_exp")
            t_pv = sem("t_pv")
            a_o, t_to = sem("a_o"), sem("t_to")
            v_rc, v_nm = sem("v_rc"), sem("v_nm")
            t_at, a_at = sem("t_at"), sem("a_at")
            g_mask = sem("g_mask")
            d_al = sem("d_al")
            v_mix = sem("v_mix")
            t_op, a_y = sem("t_op"), sem("a_y")
            mb = ps[:, 7, :]

            block = ph.enter_context(nc.Block())

            @block.sync
            def _(sp):
                def load_x(n):
                    wait_apart(sp, t_h0, 2 * n, passed)
                    sp.dma_start(lnxb[:, :, 1:S], lnx_d[bass.ds(n, 1), :, :, 0:S - 1].rearrange("o p c t -> (o p) c t")
                                 ).then_inc(d_x, 16)

                def store_h0(n):
                    wait_apart(sp, a_h0, 2 * n + 2, passed)
                    sp.dma_start(h0_d[bass.ds(n, 1), :, :].rearrange("o p m -> (o p) m"),
                                 h0[:, :, :].rearrange("p t e -> p (t e)")).then_inc(d_h0, 16)

                def store_part(n, r):
                    for g in range(3):
                        wait_apart(sp, d_st[g], 192 * n, passed)
                    sp.wait_ge((a_hi, v_mid, p_lo)[r], (4, 2, 2)[r] * (n + 1))
                    sp.dma_start(parts_d[r, :, :].rearrange("(c p) t -> p c t", p=C),
                                 part[r][:, :, :]).then_inc(d_pt[r], 16)

                def load_stacks(n, par, g, part_no):
                    wait_apart(sp, d_pt[part_no], 16 * n + 16, passed)
                    wait(sp, t_qk, STEPS * (n - 2) + 8 * (g + 1))
                    for which, parts, stack in ((0, QPARTS, qs[par]), (1, KPARTS, ks[par])):
                        for r in range(6):
                            if parts[r] == part_no:
                                rows = parts_d[part_no, which * D + 64 * g:which * D + 64 * (g + 1), :]
                                sp.dma_start(stack[HD * r:HD * (r + 1), 4 * g:4 * g + 4, :],
                                             rows.rearrange("(h d) t -> d h t", d=HD)).then_inc(d_st[g], 16)

                def load_max(n, par, lot):
                    lo, hi = LOTS[lot]
                    sp.wait_ge(v_m, 2 * n + lot + 1)
                    wait(sp, t_qk, STEPS * (n - 1))
                    for r in range(2):
                        sp.dma_start(qs[par][ST + r:ST + r + 1, lo:hi, :], mrow[lot][:, r, :]).then_inc(d_m[lot], 16)

                def store_y(n):
                    wait_apart(sp, a_y, 2 * n + 2, passed)
                    sp.dma_start(y_d[bass.ds(n, 1), :, :].rearrange("o p m -> (o p) m"),
                                 y[:, :, :].rearrange("p t e -> p (t e)")).then_inc(d_y, 16)

                def sequence(b, par, ahead=True, first=False, front=True, last=False):
                    load_max(b, par, 1)
                    if front:
                        store_h0(b + 2)
                    if ahead:
                        load_x(b + 3)
                    if front:
                        for r in range(3):
                            store_part(b + 2, r)
                            load_stacks(b + 2, par, 0, r)
                    if not last:
                        load_max(b + 1, 1 - par, 0)
                    if not first:
                        store_y(b - 1)
                    if front:
                        for g in (1, 2):
                            for r in range(3):
                                load_stacks(b + 2, par, g, r)

                sp.dma_start(ae[:, :], al_e.to_broadcast([P, 3])).then_inc(d_al, 16)
                sp.dma_start(ar[:, :], al_r.to_broadcast([P, 3])).then_inc(d_al, 16)
                sp.wait_ge(g_ones, 1)
                sp.wait_ge(d_lnx[0], 64)
                load_x(0)
                store_h0(0)
                load_x(1)
                for r in range(3):
                    store_part(0, r)
                for g in range(3):
                    for r in range(3):
                        load_stacks(0, 0, g, r)
                store_h0(1)
                load_x(2)
                for r in range(3):
                    store_part(1, r)
                for k in range(1, 4):
                    sp.wait_ge(d_lnx[k], 64)
                for g in range(3):
                    for r in range(3):
                        load_stacks(1, 1, g, r)
                load_max(0, 0, 0)
                sequence(0, 0, first=True)
                sequence(1, 1)
                with sp.Fori(1, B // 2 - 2) as it:
                    sequence(2 * it, 0)
                    sequence(2 * it + 1, 1)
                sequence(B - 4, 0)
                sequence(B - 3, 1, ahead=False)
                sequence(B - 2, 0, ahead=False, front=False)
                sequence(B - 1, 1, ahead=False, front=False, last=True)
                store_y(B - 1)
                sp.wait_ge(d_h0, 16 * B)
                sp.wait_ge(d_y, 16 * B)

            @block.gpsimd
            def _(pool):
                def norm(n):
                    pool.wait_ge(v_v2, n + 1)
                    pool.tensor_tensor(rstd2[:, :], ve2[:, :], half[:, :], ALU.pow).then_inc(p_r2, 1)

                def split(n):
                    for w in range(2):
                        pool.wait_ge(a_hi, 4 * n + 2 * w + 2)
                        wait(pool, v_mid, 2 * n)
                        pool.tensor_tensor(rest[:, 2 * w:2 * w + 2, :], x[:, 2 * w:2 * w + 2, :],
                                           part[0][:, 2 * w:2 * w + 2, :], ALU.subtract).then_inc(p_rest, 1)
                    for w in range(2):
                        pool.wait_ge(v_mid, 2 * n + w + 1)
                        wait(pool, d_pt[2], 16 * n)
                        pool.tensor_tensor(part[2][:, 2 * w:2 * w + 2, :], rest[:, 2 * w:2 * w + 2, :],
                                           part[1][:, 2 * w:2 * w + 2, :], ALU.subtract).then_inc(p_lo, 1)

                pool.memset(lnxb[:, :, 0:1], 0.0).then_inc(g_ones, 1)
                pool.wait_ge(g_ones, 1)
                pool.memset(ks[0][ST:ROWS, :, :], 1.0).then_inc(g_ones, 1)
                for k in range(2):
                    pool.wait_ge(g_ones, 2 + k)
                    pool.memset(kaug[k][:, :, :, HD:2 * HD], 1.0).then_inc(g_ones, 1)
                pool.wait_ge(g_ones, 4)
                pool.memset(hm[:, :, :], 1.0).then_inc(g_mask, 1)
                pool.wait_ge(g_mask, 1)
                pool.memset(em[:, :], 1.0).then_inc(g_mask, 1)
                pool.wait_ge(g_mask, 2)
                pool.affine_select(out=em[:, :], in_=em[:, :], compare_op=ALU.is_ge, fill=0.0,
                                   base=EMBED[1] - C - 1, pattern=[[0, 1]], channel_multiplier=-1).then_inc(g_mask, 1)
                for ij in range(9):
                    pool.wait_ge(g_mask, 3 + ij)
                    pool.affine_select(out=hm[:, ij, :], in_=hm[:, ij, :], compare_op=ALU.is_ge, fill=0.0,
                                       base=RATIO[ij % 3] * EMBED[ij // 3] - 1, pattern=[[-P, HC]],
                                       channel_multiplier=-1).then_inc(g_mask, 1)
                pool.wait_ge(g_mask, 12)
                for n in range(2):
                    norm(n)
                    split(n)
                for k in range(4):
                    pool.wait_ge(d_lnx[k], 64)
                pool.wait_ge(p_lo, 4)
                pool.memset(ks[1][ST:ROWS, :, :], 1.0).then_inc(g_ones, 1)
                pool.wait_ge(g_ones, 5)
                norm(2)
                split(2)
                with pool.Fori(3, B) as n:
                    norm(n)
                    split(n)

            @block.scalar
            def _(act):
                def h0_copy(n, i):
                    act.wait_ge(t_h0, 2 * n + i + 1)
                    if i == 0:
                        wait(act, v_z, NT * n)
                        wait(act, d_h0, 16 * n)
                    act.copy(h0[:, 2 * i:2 * i + 2, :],
                             mb[:, 0:2 * D].rearrange("p (t e) -> p t e", t=2)).then_inc(a_h0, 1)

                def zT_copy(n, c):
                    act.wait_ge(t_zt, 2 * n + c + 1)
                    wait(act, t_pr, 4 * n)
                    act.copy(zT[:, c, :], mb[0:C, :]).then_inc(a_zt, 1)

                def x_copy(n, c):
                    act.wait_ge(t_pr, 4 * n + c + 1)
                    if c == 0:
                        wait(act, p_rest, 2 * n)
                        wait(act, t_kt, 2 * n)
                        wait(act, d_pt[0], 16 * n)
                    act.copy(x[:, c, :], mb[0:C, :]).then_inc(a_x, 1)
                    act.copy(part[0][:, c, :], mb[0:C, :]).then_inc(a_hi, 1)

                def k_copy(n, par, c):
                    act.wait_ge(t_kt, 2 * n + c + 1)
                    wait(act, t_pv, 6 * (n - 1))
                    act.copy(kaug[par][:, :, 6 * c:6 * c + 6, 0:HD],
                             mb[:, 0:NT * C].rearrange("p (t h d) -> p t h d", t=NT, h=6)).then_inc(a_kt, 1)

                def y_copy(n, i):
                    act.wait_ge(t_op, 2 * n + i + 1)
                    wait(act, d_y, 16 * n)
                    act.copy(y[:, 2 * i:2 * i + 2, :],
                             mb[:, 0:2 * D].rearrange("p (t e) -> p t e", t=2)).then_inc(a_y, 1)

                def exp(b, s):
                    u = s // 4
                    act.wait_ge(t_qk, STEPS * b + s + 1)
                    if s % 4 == 0:
                        wait(act, t_pv, 6 * b + u - 1)
                    act.activation(E[:, u % 2, s % 4, :, :], ps[:, 2 * (s % 2):2 * (s % 2) + 2, :], ACT.Exp,
                                   scale=SCALE).then_inc(a_exp, 1)

                def o_copy(n, g):
                    act.wait_ge(t_pv, 6 * n + 2 * g + 2)
                    wait(act, t_to, 3 * n + g)
                    act.copy(o[:, :], ps[:, 6, :]).then_inc(a_o, 1)

                def aT_copy(n, c):
                    act.wait_ge(t_at, 2 * n + c + 1)
                    wait(act, t_op, 2 * n)
                    act.copy(aT[:, c, :], mb[0:C, :]).then_inc(a_at, 1)

                def sequence(b, par, main=True, first=False, front=True, last=False):
                    for s in range(STEPS):
                        if main:
                            exp(b, s)
                            if s in (VALUES_AT[1], VALUES_AT[3]):
                                o_copy(b, s // 8 - 1)
                        if s == LAST_VALUES_AT and not first:
                            o_copy(b - 1, 2)
                        if s in H0_AT and front:
                            h0_copy(b + 2, s - H0_AT[0])
                        if s in KEYS_AT and not last:
                            k_copy(b + 1, 1 - par, s - KEYS_AT[0])
                        if s in NORM_AT and front:
                            zT_copy(b + 2, s - NORM_AT[0])
                        if s in PROJECT_AT and front:
                            x_copy(b + 2, s - PROJECT_AT[0])
                        if s in HEADS_AT and not first:
                            aT_copy(b - 1, s - HEADS_AT[0])
                        if s in OUT_AT and not first:
                            y_copy(b - 1, s - OUT_AT[0])

                act.wait_ge(g_ones, 4)
                for i in range(2):
                    h0_copy(0, i)
                for c in range(2):
                    zT_copy(0, c)
                for c in range(4):
                    x_copy(0, c)
                sequence(-1, 1, main=False, first=True)
                for k in range(4):
                    act.wait_ge(d_lnx[k], 64)
                sequence(0, 0, first=True)
                sequence(1, 1)
                with act.Fori(1, B // 2 - 2) as it:
                    sequence(2 * it, 0)
                    sequence(2 * it + 1, 1)
                sequence(B - 4, 0)
                sequence(B - 3, 1)
                sequence(B - 2, 0, front=False)
                sequence(B - 1, 1, front=False, last=True)
                o_copy(B - 1, 2)
                for c in range(2):
                    aT_copy(B - 1, c)
                for i in range(2):
                    y_copy(B - 1, i)

            @block.vector
            def _(dve):
                def norm(n, i):
                    dve.wait_ge(a_h0, 2 * n + i + 1)
                    for t in (2 * i, 2 * i + 1):
                        dve.bn_stats(st2[:, t, :], h0[:, t, :]).then_inc(v_s2, 1)
                    if i == 1:
                        wait_apart(dve, v_s2, NT * n + NT, passed)
                        for t in range(NT):
                            dve.bn_aggr(mv2[:, t, :], st2[:, t, :]).then_inc(v_a2, 1)
                        dve.wait_ge(v_a2, NT * n + NT)
                        dve.tensor_scalar(ve2[:, :], mv2[:, :, 1], EPS, None, ALU.add).then_inc(v_v2, 1)

                def normalise(n):
                    dve.wait_ge(p_r2, n + 1)
                    wait(dve, t_zt, 2 * n)
                    for t in range(NT):
                        dve.tensor_scalar(z[:, t, :], h0[:, t, :], mv2[:, t, 0:1], rstd2[:, t:t + 1],
                                          ALU.subtract, ALU.mult).then_inc(v_z, 1)

                def middle(n, w):
                    dve.wait_ge(p_rest, 2 * n + w + 1)
                    wait(dve, d_pt[1], 16 * n)
                    dve.tensor_copy(part[1][:, 2 * w:2 * w + 2, :], rest[:, 2 * w:2 * w + 2, :]).then_inc(v_mid, 1)

                def maxima(n, k):
                    dve.wait_ge(t_mx, MAXIMA * n + k + 1)
                    if k % (8 * NT) == 0:
                        wait(dve, t_mt, 2 * n - 1 + k // (8 * NT))
                    dve.tensor_reduce(mx[:, k % NT, k // NT:k // NT + 1], ps[:, 4 + k % 2, :], AX_X,
                                      ALU.max).then_inc(v_mx, 1)

                def max_rows(n, lot):
                    rows, heads = mrow[lot], LOTS[lot][1] - LOTS[lot][0]
                    dve.wait_ge(t_mt, 2 * n + lot + 1)
                    wait(dve, d_m[lot], 32 * n)
                    dve.tensor_scalar(rows[:, 0, :], mb[0:heads, :], -1.0, None, ALU.mult).then_inc(v_mh, 1)
                    dve.wait_ge(v_mh, 2 * n + lot + 1)
                    dve.scalar_tensor_tensor(out=rows[:, 1, :], in0=mb[0:heads, :], scalar=-1.0, in1=rows[:, 0, :],
                                             op0=ALU.mult, op1=ALU.subtract).then_inc(v_m, 1)

                def weigh(n, g):
                    heads = mb[:, :].rearrange("p (t h c) -> p t h c", t=NT, h=4)
                    dve.wait_ge(t_to, 3 * n + g + 1)
                    dve.reciprocal(recip[:, :, :, :], heads[:, :, :, HD:HD + 1]).then_inc(v_rc, 1)
                    dve.wait_ge(v_rc, 3 * n + g + 1)
                    wait(dve, t_at, 2 * n)
                    dve.tensor_tensor(at[:, :, 64 * g:64 * (g + 1)].rearrange("p t (h d) -> p t h d", h=4),
                                      heads[:, :, :, 0:HD], recip[:, :, :, :].to_broadcast([P, NT, 4, HD]),
                                      ALU.mult).then_inc(v_nm, 1)

                chain = [0]

                def step(ins):
                    chain[0] += 1
                    ins.then_inc(v_mix, 1)
                    dve.wait_ge(v_mix, chain[0])

                def mix_start():
                    dve.wait_ge(d_al, 32)
                    dve.wait_ge(g_mask, 12)
                    for i in range(3):
                        step(dve.tensor_scalar(a[:, 3 * i:3 * i + 3], ar[:, :], ae[:, i:i + 1], None, ALU.mult))
                    step(dve.memset(c0[:, :, :], 0.0))
                    step(dve.memset(c1[:, :, :], 0.0))
                    step(dve.memset(c0b[:, :], 0.0))
                    step(dve.memset(c1b[:, :], 0.0))
                    step(dve.tensor_scalar(ema[:, :], a[0:C, :], em[:, 0:1], None, ALU.mult))
                    for ij in range(9):
                        step(dve.tensor_scalar(hma[:, ij, :], hm[:, ij, :], a[:, ij:ij + 1], None, ALU.mult))

                def mix(ij):
                    i, j = ij // 3, ij % 3
                    e, h = EMBED[i], RATIO[j] * EMBED[i]
                    dve.tensor_scalar(c0[:, 0, 0:h], c0[:, 0, 0:h], a[0:C, ij:ij + 1], None, ALU.add)
                    if i:
                        upper = a[0:C, ij:ij + 1] if i == 2 else ema[:, ij:ij + 1]
                        dve.tensor_scalar(c0[:, 1, 0:h], c0[:, 1, 0:h], upper, None, ALU.add)
                    for k in range((h + P - 1) // P):
                        dve.tensor_scalar(c1[:, k, 0:e], c1[:, k, 0:e], hma[:, ij, k:k + 1], None, ALU.add)
                    dve.tensor_tensor(c0b[:, :], c0b[:, :], hma[:, ij, :], ALU.add)
                    step(dve.tensor_scalar(c1b[:, 0:e], c1b[:, 0:e], a[:, ij:ij + 1], None, ALU.add))

                def mix_end():
                    dve.wait_ge(d_ffn, 16 * 4)
                    dve.tensor_tensor(w0[:, :, :], w0[:, :, :], c0[:, :, :], ALU.mult)
                    dve.tensor_tensor(w1[:, :, :], w1[:, :, :], c1[:, :, :], ALU.mult)
                    dve.tensor_tensor(b0[:, :], b0[:, :], c0b[:, :], ALU.mult)
                    step(dve.tensor_tensor(b1[:, :], b1[:, :], c1b[:, :], ALU.mult))

                def sequence(b, par, main=True, first=False, front=True, last=False):
                    k = 0
                    for s in range(STEPS):
                        counts = (MAX_AT if main else MAX_ALONE)[s]
                        for place in range(5):
                            if place == 4:
                                if s == LATE_MAX_AT and main:
                                    max_rows(b, 1)
                                if s in (H0_AT[1], H0_AT[1] + 1) and front:
                                    norm(b + 2, s - H0_AT[1])
                                if s == H0_AT[1] + 2 and front:
                                    normalise(b + 2)
                                if s == LAST_SUMS_AT and not first:
                                    weigh(b - 1, 2)
                                if s in (PROJECT_AT[3], PROJECT_AT[3] + 2) and front:
                                    middle(b + 2, (s - PROJECT_AT[3]) // 2)
                                if s in SUMS_AT and main:
                                    weigh(b, SUMS_AT.index(s))
                                if s == EARLY_MAX_AT and not last:
                                    max_rows(b + 1, 0)
                            if not last:
                                for _ in range(counts[place]):
                                    maxima(b + 1, k)
                                    k += 1
                        if main and first and s % 2 == 0:
                            if s == 4:
                                mix_start()
                            if 6 <= s < 24:
                                mix(s // 2 - 3)

                for i in range(2):
                    norm(0, i)
                normalise(0)
                for w in range(2):
                    middle(0, w)
                sequence(-1, 1, main=False, first=True)
                sequence(0, 0, first=True)
                mix_end()
                sequence(1, 1)
                with dve.Fori(1, B // 2 - 2) as it:
                    sequence(2 * it, 0)
                    sequence(2 * it + 1, 1)
                sequence(B - 4, 0)
                sequence(B - 3, 1)
                sequence(B - 2, 0, front=False)
                sequence(B - 1, 1, front=False, last=True)
                weigh(B - 1, 2)

            @block.tensor
            def _(pe):
                def h0_tiles(n, i, t):
                    if t == 0:
                        if i == 0:
                            pe.wait_ge(d_x, 16 * n + 16)
                        else:
                            pe.wait_ge(a_h0, 2 * n + 1)
                    for c in range(2):
                        last = pe.matmul(mb[:, t * D:(t + 1) * D], lnxb[:, c, (2 * i + t) * P:(2 * i + t + 1) * P],
                                         M[:, c, :], start=(c == 0), stop=(c == 1))
                    if t == 1:
                        last.then_inc(t_h0, 1)

                def z_transpose(n, c):
                    if c == 0:
                        pe.wait_ge(v_z, NT * n + NT)
                    else:
                        pe.wait_ge(a_zt, 2 * n + 1)
                    for t in range(NT):
                        last = pe.transpose(mb[0:C, t * P:(t + 1) * P], z[:, t, c * C:(c + 1) * C], ident[:, :])
                    last.then_inc(t_zt, 1)

                def project(n, c, k):
                    if k == 0:
                        if c == 0:
                            pe.wait_ge(a_zt, 2 * n + 2)
                        else:
                            pe.wait_ge(a_hi, 4 * n + c)
                    last = pe.matmul(mb[0:C, :], wqk_s[:, k, c * C:(c + 1) * C], zT[:, k, :],
                                     start=(k == 0), stop=(k == 1))
                    if k == 1:
                        last.then_inc(t_pr, 1)

                def k_transpose(n, c):
                    if c == 0:
                        pe.wait_ge(a_x, 4 * n + 4)
                    else:
                        pe.wait_ge(a_kt, 2 * n + 1)
                    for t in range(NT):
                        last = pe.transpose(mb[:, t * C:(t + 1) * C], x[:, 2 + c, t * P:(t + 1) * P], ident[0:C, 0:C])
                    last.then_inc(t_kt, 1)

                def max_scores(n, par, k):
                    h, t = k // NT, k % NT
                    if k % (4 * NT) == 0:
                        pe.wait_ge(d_st[h // 4], 192 * n + 192)
                    wait(pe, v_mx, MAXIMA * n + k - 1)
                    pe.matmul(ps[:, 4 + k % 2, :], qs[par][0:ST, h, t * P:(t + 1) * P], ks[par][0:ST, h, :],
                              start=True, stop=True).then_inc(t_mx, 1)

                def max_transpose(n, lot):
                    lo, hi = LOTS[lot]
                    pe.wait_ge(v_mx, MAXIMA * n + NT * hi)
                    for t in range(NT):
                        last = pe.transpose(mb[0:hi - lo, t * P:(t + 1) * P], mx[:, t, lo:hi], ident[:, :])
                    last.then_inc(t_mt, 1)

                def scores(b, par, s):
                    h = 4 * (s // 8) + s % 4
                    if s in (0, 16):
                        pe.wait_ge(d_m[s // 16], 32 * b + 32)
                    wait(pe, a_exp, STEPS * b + s - 1)
                    for i in range(2):
                        t = 2 * (s // 4 % 2) + i
                        last = pe.matmul(ps[:, 2 * (s % 2) + i, :], ks[par][0:ROWS, h, t * P:(t + 1) * P],
                                         qs[par][0:ROWS, h, :], start=True, stop=True)
                    last.then_inc(t_qk, 1)

                def values(b, par, u, i):
                    if i == 0:
                        if u == 0:
                            pe.wait_ge(a_kt, 2 * b + 2)
                        if u % 2 == 0:
                            wait(pe, a_o, 3 * b + u // 2)
                        pe.wait_ge(a_exp, STEPS * b + 4 * u + 4)
                    t = 2 * (u % 2) + i
                    for j in range(4):
                        last = pe.matmul(ps[32 * j:32 * j + 32, 6, :], kaug[par][:, t, 4 * (u // 2) + j, :],
                                         E[:, u % 2, j, i, :], start=(t == 0), stop=(t == NT - 1))
                    if i == 1:
                        last.then_inc(t_pv, 1)

                def o_transpose(n, g):
                    pe.wait_ge(a_o, 3 * n + g + 1)
                    for t in range(NT):
                        last = pe.transpose(mb[:, t * P:(t + 1) * P], o[:, t * P:(t + 1) * P], ident[:, :])
                    last.then_inc(t_to, 1)

                def a_transpose(n, c):
                    if c == 0:
                        pe.wait_ge(v_nm, 3 * n + 3)
                    else:
                        pe.wait_ge(a_at, 2 * n + 1)
                    for t in range(NT):
                        last = pe.transpose(mb[0:C, t * P:(t + 1) * P], at[:, t, c * C:(c + 1) * C], ident[:, :])
                    last.then_inc(t_at, 1)

                def out_tiles(n, i, t):
                    if t == 0:
                        if i == 0:
                            pe.wait_ge(a_at, 2 * n + 2)
                        else:
                            pe.wait_ge(a_y, 2 * n + 1)
                    for c in range(2):
                        last = pe.matmul(mb[:, t * D:(t + 1) * D], aT[:, c, (2 * i + t) * P:(2 * i + t + 1) * P],
                                         wout_s[:, c, :], start=(c == 0), stop=(c == 1))
                    if t == 1:
                        last.then_inc(t_op, 1)

                def sequence(b, par, main=True, first=False, front=True, last=False):
                    k = 0
                    for s in range(STEPS):
                        counts = (MAX_AT if main else MAX_ALONE)[s]

                        def max_products(place):
                            if not last:
                                for j in range(counts[place]):
                                    max_scores(b + 1, 1 - par, k + sum(counts[:place]) + j)

                        if main:
                            scores(b, par, s)
                        max_products(0)
                        for i in range(2):
                            if s in VALUES_AT and main:
                                values(b, par, VALUES_AT.index(s), i)
                            if s == LAST_VALUES_AT and not first:
                                values(b - 1, 1 - par, 5, i)
                            max_products(1 + i)
                        if s == LATE_MAX_AT and main:
                            if first:
                                pe.wait_ge(v_m, 2 * b + 1)
                            else:
                                pe.wait_ge(v_nm, 3 * b - 1)
                            max_transpose(b, 1)
                        if s in H0_AT and front:
                            if s == H0_AT[0]:
                                if main:
                                    pe.wait_ge(v_m, 2 * b + 2)
                                else:
                                    pe.wait_ge(a_hi, 4)
                            h0_tiles(b + 2, s - H0_AT[0], 0)
                            max_products(3)
                            h0_tiles(b + 2, s - H0_AT[0], 1)
                        if s in KEYS_AT and not last:
                            if front:
                                pe.wait_ge(a_h0, 2 * (b + 2) + 2)
                            else:
                                pe.wait_ge(v_m, 2 * b + 2)
                            k_transpose(b + 1, s - KEYS_AT[0])
                        if s == LAST_SUMS_AT and not first:
                            if last:
                                pe.wait_ge(v_m, 2 * b + 2)
                            else:
                                pe.wait_ge(a_kt, 2 * (b + 1) + 2)
                            o_transpose(b - 1, 2)
                        if s in NORM_AT and front:
                            if first:
                                pe.wait_ge(a_kt, 2 * (b + 1) + 2)
                            else:
                                pe.wait_ge(v_nm, 3 * b)
                            z_transpose(b + 2, s - NORM_AT[0])
                        if s in PROJECT_AT and front:
                            project(b + 2, s - PROJECT_AT[0], 0)
                            max_products(3)
                            project(b + 2, s - PROJECT_AT[0], 1)
                        if s in HEADS_AT and not first:
                            if front:
                                pe.wait_ge(a_hi, 4 * (b + 2) + 4)
                            a_transpose(b - 1, s - HEADS_AT[0])
                        if s == SUMS_AT[0] and main:
                            if first:
                                pe.wait_ge(a_hi, 4 * (b + 2) + 4)
                            else:
                                pe.wait_ge(a_at, 2 * b)
                            o_transpose(b, 0)
                        if s in OUT_AT and not first:
                            pe.wait_ge(v_nm, 3 * b + 1)
                            out_tiles(b - 1, s - OUT_AT[0], 0)
                            max_products(3)
                            out_tiles(b - 1, s - OUT_AT[0], 1)
                        if s == EARLY_MAX_AT and not last:
                            if not main:
                                pe.wait_ge(a_hi, 4 * (b + 2) + 4)
                            elif first:
                                pe.wait_ge(v_nm, 3 * b + 1)
                            else:
                                pe.wait_ge(a_y, 2 * b)
                            max_transpose(b + 1, 0)
                        if s == SUMS_AT[1] and main:
                            if last:
                                pe.wait_ge(a_y, 2 * b)
                            else:
                                pe.wait_ge(v_m, 2 * b + 3)
                            o_transpose(b, 1)
                        if (s in H0_AT + PROJECT_AT and not front) or (s in OUT_AT and first):
                            max_products(3)
                        max_products(4)
                        k += sum(counts)

                pe.wait_ge(g_ones, 4)
                for i in range(2):
                    for t in range(2):
                        h0_tiles(0, i, t)
                for c in range(2):
                    z_transpose(0, c)
                for c in range(4):
                    for k in range(2):
                        project(0, c, k)
                sequence(-1, 1, main=False, first=True)
                pe.wait_ge(g_ones, 5)
                sequence(0, 0, first=True)
                sequence(1, 1)
                with pe.Fori(1, B // 2 - 2) as it:
                    sequence(2 * it, 0)
                    sequence(2 * it + 1, 1)
                sequence(B - 4, 0)
                sequence(B - 3, 1)
                sequence(B - 2, 0, front=False)
                sequence(B - 1, 1, front=False, last=True)
                for i in range(2):
                    values(B - 1, 1, 5, i)
                pe.wait_ge(v_nm, 3 * B - 1)
                o_transpose(B - 1, 2)
                for c in range(2):
                    a_transpose(B - 1, c)
                for i in range(2):
                    for t in range(2):
                        out_tiles(B - 1, i, t)

        with ExitStack() as ph:
            hin = [sb(f"hin{k}", [P, NT, D], F32, ph) for k in range(2)]
            yin = [sb(f"yin{k}", [P, NT, D], F32, ph) for k in range(2)]
            hs = sb("hs", [P, NT, D], F32, ph)
            hb = [sb(f"hb{k}", [P, NT, D], F32, ph) for k in range(2)]
            fz = sb("fz", [P, NT, D], F32, ph)
            st3 = sb("st3", [P, NT, 6], F32, ph)
            mv3 = sb("mv3", [P, NT, 2], F32, ph)
            ve3 = sb("ve3", [P, NT], F32, ph)
            rstd3 = sb("rstd3", [P, NT], F32, ph)
            fzT = [sb(f"fzT{k}", [C, 2, S], F32, ph) for k in range(2)]
            act_s = [sb(f"act{k}", [P, HC, S], F32, ph) for k in range(2)]
            res = [sb(f"res{k}", [P, NT, D], F32, ph) for k in range(2)]

            f_ld = [sem(f"f_ld{k}") for k in range(2)]
            f_out = [sem(f"f_out{k}") for k in range(2)]
            f_h = sem("f_h")
            f_st, f_ag, f_var, f_rstd = sem("f_st"), sem("f_ag"), sem("f_var"), sem("f_rstd")
            f_z = sem("f_z")
            f_hb = sem("f_hb")
            f_zt, f_zc = sem("f_zt"), sem("f_zc")
            f_up, f_act = sem("f_up"), sem("f_act")
            f_dn, f_res = sem("f_dn"), sem("f_res")

            block = ph.enter_context(nc.Block())

            @block.sync
            def _(sp):
                def load(n, k):
                    wait(sp, f_h, n - 1)
                    for to, of in ((hin[k], h0_d), (yin[k], y_d)):
                        sp.dma_start(to[:, :, :].rearrange("p t e -> p (t e)"),
                                     of[bass.ds(n, 1), :, :].rearrange("o p m -> (o p) m")).then_inc(f_ld[k], 16)

                def store(n, k):
                    wait_apart(sp, f_res, 2 * n + 2, passed)
                    sp.dma_start(out[bass.ds(n, 1), :, :].rearrange("o (t p) e -> p (o t) e", p=P),
                                 res[k][:, :, :]).then_inc(f_out[k], 16)

                load(0, 0)
                load(1, 1)
                with sp.Fori(0, B // 2 - 1) as it:
                    for k in range(2):
                        load(2 * it + k + 2, k)
                        store(2 * it + k, k)
                for k in range(2):
                    store(B - 2 + k, k)
                for k in range(2):
                    sp.wait_ge(f_out[k], 16 * (B // 2))

            @block.gpsimd
            def _(pool):
                with pool.Fori(0, B // 2) as it:
                    for k in range(2):
                        n = 2 * it + k
                        pool.wait_ge(f_var, n + 1)
                        pool.tensor_tensor(rstd3[:, :], ve3[:, :], half[:, :], ALU.pow).then_inc(f_rstd, 1)
                        for t in range(NT):
                            pool.tensor_tensor(hb[k][:, t, :], hs[:, t, :], b1[:, :], ALU.add).then_inc(f_hb, 1)

            @block.scalar
            def _(act):
                def z_copy(n, k, c):
                    act.wait_ge(f_zt, 2 * n + c + 1)
                    act.copy(fzT[k][:, c, :], ps[0:C, 4 + c, :]).then_inc(f_zc, 1)

                def gelu(n, k, m):
                    act.wait_ge(f_up, HC * n + m + 1)
                    if m == 0:
                        wait(act, f_dn, 2 * (n - 1))
                    act.activation(act_s[k][:, m, :], ps[:, (2 * k + m) % 4, :], ACT.Gelu_apprx_tanh,
                                   bias=b0[:, m:m + 1]).then_inc(f_act, 1)

                def sequence(n, k, last=False):
                    for m in range(HC):
                        gelu(n, k, m)
                        if m in (3, 4) and not last:
                            z_copy(n + 1, 1 - k, m - 3)

                for c in range(2):
                    z_copy(0, 0, c)
                sequence(0, 0)
                sequence(1, 1)
                with act.Fori(1, B // 2 - 1) as it:
                    sequence(2 * it, 0)
                    sequence(2 * it + 1, 1)
                sequence(B - 2, 0)
                sequence(B - 1, 1, last=True)

            @block.vector
            def _(dve):
                def norm(n, k):
                    dve.wait_ge(f_ld[k], 16 * (n - k) + 32)
                    wait(dve, f_hb, NT * n)
                    wait(dve, f_z, NT * n)
                    dve.tensor_tensor(hs[:, :, :], hin[k][:, :, :], yin[k][:, :, :], ALU.add).then_inc(f_h, 1)
                    dve.wait_ge(f_h, n + 1)
                    for t in range(NT):
                        dve.bn_stats(st3[:, t, :], hs[:, t, :]).then_inc(f_st, 1)
                    wait_apart(dve, f_st, NT * n + NT, passed)
                    for t in range(NT):
                        dve.bn_aggr(mv3[:, t, :], st3[:, t, :]).then_inc(f_ag, 1)
                    dve.wait_ge(f_ag, NT * n + NT)
                    dve.tensor_scalar(ve3[:, :], mv3[:, :, 1], EPS, None, ALU.add).then_inc(f_var, 1)
                    dve.wait_ge(f_rstd, n + 1)
                    wait(dve, f_zt, 2 * n)
                    for t in range(NT):
                        dve.tensor_scalar(fz[:, t, :], hs[:, t, :], mv3[:, t, 0:1], rstd3[:, t:t + 1],
                                          ALU.subtract, ALU.mult).then_inc(f_z, 1)

                def result(n, k, i):
                    dve.wait_ge(f_dn, 2 * n + i + 1)
                    if i == 0:
                        dve.wait_ge(f_hb, NT * n + NT)
                        wait(dve, f_out[k], 8 * (n - k))
                    dve.tensor_tensor(res[k][:, 2 * i:2 * i + 2, :],
                                      ps[:, 6 + i, 0:2 * D].rearrange("p (t e) -> p t e", t=2),
                                      hb[k][:, 2 * i:2 * i + 2, :], ALU.add).then_inc(f_res, 1)

                norm(0, 0)
                norm(1, 1)
                for k in range(2):
                    for i in range(2):
                        result(k, k, i)
                    norm(2 + k, k)
                with dve.Fori(1, B // 2 - 1) as it:
                    for k in range(2):
                        for i in range(2):
                            result(2 * it + k, k, i)
                        norm(2 * it + k + 2, k)
                for k in range(2):
                    for i in range(2):
                        result(B - 2 + k, k, i)

            @block.tensor
            def _(pe):
                def z_transpose(n, k, c):
                    pe.wait_ge(f_z, NT * n + NT)
                    wait(pe, f_zc, 2 * n)
                    for t in range(NT):
                        last = pe.transpose(ps[0:C, 4 + c, t * P:(t + 1) * P], fz[:, t, c * C:(c + 1) * C], ident[:, :])
                    last.then_inc(f_zt, 1)

                def up(n, k, m):
                    if m == 0:
                        pe.wait_ge(f_zc, 2 * n + 2)
                    wait(pe, f_act, HC * n + m - 3)
                    for c in range(2):
                        last = pe.matmul(ps[:, (2 * k + m) % 4, :], w0[:, c, m * P:(m + 1) * P], fzT[k][:, c, :],
                                         start=(c == 0), stop=(c == 1))
                    last.then_inc(f_up, 1)

                def down(n, k, i):
                    wait(pe, f_res, 2 * (n - 1) + i + 1)
                    for t in range(2):
                        for m in range(HC):
                            if i == 0 and t == 0:
                                pe.wait_ge(f_act, HC * n + m + 1)
                            last = pe.matmul(ps[:, 6 + i, t * D:(t + 1) * D],
                                             act_s[k][:, m, (2 * i + t) * P:(2 * i + t + 1) * P], w1[:, m, :],
                                             start=(m == 0), stop=(m == HC - 1))
                    last.then_inc(f_dn, 1)

                def sequence(n, k, last=False):
                    for m in range(HC):
                        up(n, k, m)
                        if m in (3, 4) and not last:
                            z_transpose(n + 1, 1 - k, m - 3)
                    for i in range(2):
                        down(n, k, i)

                for c in range(2):
                    z_transpose(0, 0, c)
                sequence(0, 0)
                sequence(1, 1)
                with pe.Fori(1, B // 2 - 1) as it:
                    sequence(2 * it, 0)
                    sequence(2 * it + 1, 1)
                sequence(B - 2, 0)
                sequence(B - 1, 1, last=True)


def layouts(x, wte, W_proj, ln_w, ln_b, W_val, W_out, trace0, w_qkv, w_out, w_fc, b_fc, w_proj, b_proj, ae, ar):
    chunks = lambda w: np.ascontiguousarray(w.reshape(2, C, -1).transpose(1, 0, 2))
    pieces = x.reshape(B * CH, TS)
    ids = np.concatenate([pieces, np.roll(pieces, -1, axis=0)[:, :LAG]], axis=1)
    return {
        "ids": np.ascontiguousarray(ids), "wte": wte,
        "wpT": chunks(W_proj.T), "wvT": chunks(W_val.T),
        "wpN": np.ascontiguousarray(W_proj.reshape(TH, TD, D).transpose(1, 0, 2)),
        "woT": np.ascontiguousarray(W_out.T.reshape(TH, TD, D).transpose(1, 0, 2)),
        "t0T": np.ascontiguousarray(trace0.transpose(2, 0, 1)),
        "lnw": np.ascontiguousarray(ln_w.reshape(2, C).T), "lnb": np.ascontiguousarray(ln_b.reshape(2, C).T),
        "wqk": chunks(w_qkv[:, :2 * D]), "wout": chunks(w_out),
        "w0T": chunks(w_fc.T), "bfc": np.ascontiguousarray(b_fc.reshape(HC, P).T),
        "w1T": np.ascontiguousarray(w_proj.T.reshape(HC, P, D).transpose(1, 0, 2)), "bproj": b_proj.reshape(1, D),
        "al_e": ae.reshape(1, 3), "al_r": ar.reshape(1, 3),
    }


_INS = ['x', 'L0_tok_wte', 'L0_tok_W_proj', 'L0_tok_ln_w', 'L0_tok_ln_b', 'L0_tok_W_val', 'L0_tok_W_out',
        'L0_tok_trace0', 'L0_attn_w_qkv', 'L0_attn_w_out', 'L0_ffn_w_fc', 'L0_ffn_b_fc', 'L0_ffn_w_proj',
        'L0_ffn_b_proj', 'L0_ffn_alpha_e', 'L0_ffn_alpha_r']


def kernel(**inputs):
    import concourse.bacc as bacc
    from concourse.bass_utils import run_bass_kernel_spmd

    arrays = layouts(*(np.asarray(inputs[name]) for name in _INS))
    nc = bacc.Bacc("TRN2", target_bir_lowering=False, num_devices=1)
    ins = {k: nc.dram_tensor(k, v.shape, mybir.dt.from_np(v.dtype), kind="ExternalInput").ap()
           for k, v in arrays.items()}
    out = nc.dram_tensor("out", (B, S, D), F32, kind="ExternalOutput").ap()
    tower(nc, *ins.values(), out)
    r = run_bass_kernel_spmd(nc, [arrays], core_ids=[0])
    return r.results[0]["out"]
```

```python
from contextlib import ExitStack

import numpy as np
import concourse.bass as bass
from concourse import mybir

F32 = mybir.dt.float32
BF16 = mybir.dt.bfloat16
F32R = mybir.dt.float32r
I32 = mybir.dt.int32
ACT = mybir.ActivationFunctionType
ALU = mybir.AluOpType
AX_X = mybir.AxisListType.X

P = 128
B, S, D = 16, 512, 192
C = D // 2
CH = 8
TS = S // CH
LAG = 2
NG = TS // 4
NR = NG // 2
TH, TD = 8, 64
NH, HD = 12, 16
NT = S // P
HID, HC = 768, 6
EPS = 1e-5
DECAY = 0.99
UPDATE = 0.1 / (B * (S - LAG))
SCALE = float(D) ** -0.5
EMBED = [96, 144, 192]
RATIO = [2, 3, 4]
QPARTS = [0, 0, 1, 0, 1, 2]
KPARTS = [0, 1, 0, 2, 1, 0]
ST = 6 * HD
MAXIMA = NH * NT
STEPS = 24
LATE_MAX_AT = 0
H0_AT = (1, 2)
KEYS_AT = (3, 4)
NORM_AT = (5, 6)
PROJECT_AT = (8, 10, 11, 12)
LAST_SUMS_AT = 9
SUMS_AT = (13, 21)
HEADS_AT = (14, 15)
OUT_AT = (16, 19)
EARLY_MAX_AT = 17
VALUES_AT = (6, 10, 14, 18, 22)
LAST_VALUES_AT = 1
MAX_AT = [(int(s != KEYS_AT[0]), int(s in VALUES_AT + (LAST_VALUES_AT,)), int(s in VALUES_AT + (LAST_VALUES_AT,)),
           int(s in H0_AT + PROJECT_AT + OUT_AT), int(s in PROJECT_AT + (SUMS_AT[1] - 2,))) for s in range(STEPS)]
assert sum(sum(counts) for counts in MAX_AT) == MAXIMA
MAX_ALONE = [(0, 0, 0, 2, 2) if s in PROJECT_AT else (0, 0, 0, 0, 16 * (abs(s - EARLY_MAX_AT) == 1))
             for s in range(STEPS)]
LOTS = [(0, 8), (8, NH)]
MIX_STEPS = 17 + 9 + 1


def wait(eng, sem, value):
    if not (isinstance(value, int) and value <= 0):
        eng.wait_ge(sem, value)


def wait_apart(eng, sem, value, passed):
    wait(eng, sem, value)
    if not isinstance(value, int):
        eng.sem_inc(passed, 1)


def tower(nc, ids, wte, wpT, wvT, wpN, woT, t0T, lnw, lnb, wqk, wout, w0T, bfc, w1T, bproj,
          al_e, al_r, out):
    lnx_d = nc.dram_tensor("lnx_d", [B, C, 2, S], F32).ap()
    parts_d = nc.dram_tensor("parts_d", [3, 4 * C, S], BF16).ap()
    h0_d = nc.dram_tensor("h0_d", [B, P, NT * D], F32).ap()
    y_d = nc.dram_tensor("y_d", [B, P, NT * D], F32).ap()

    with ExitStack() as top:
        def sb(name, shape, dt, ctx=top):
            return ctx.enter_context(nc.sbuf_tensor(name, shape, dt))

        def sem(name):
            return top.enter_context(nc.semaphore(name))

        ps = top.enter_context(nc.psum_tensor("ps", [P, 8, 512], F32))
        ident = sb("ident", [P, P], F32)
        M = sb("M", [C, 2, D], F32)
        w0 = sb("w0", [C, 2, HID], F32)
        w0_hi = sb("w0_hi", [C, 2, HID], F32R)
        w0_lo = sb("w0_lo", [C, 2, HID], F32R)
        wqk_hi = sb("wqk_hi", [C, 2, 2 * D], F32R)
        wqk_lo = sb("wqk_lo", [C, 2, 2 * D], F32R)
        w1 = sb("w1", [P, HC, D], F32)
        b0 = sb("b0", [P, HC], F32)
        b1 = sb("b1", [P, D], F32)
        wout_s = sb("wout_s", [C, 2, D], F32)
        half = sb("half", [P, 8], F32)
        lnxb = sb("lnxb", [C, 2, S], F32)
        ae = sb("ae", [P, 3], F32)
        ar = sb("ar", [P, 3], F32)
        a = sb("a", [P, 9], F32)
        hm = sb("hm", [P, 9, HC], F32)
        em = sb("em", [C, 1], F32)
        hma = sb("hma", [P, 9, HC], F32)
        ema = sb("ema", [C, 9], F32)
        c0 = sb("c0", [C, 2, HID], F32)
        c1 = sb("c1", [P, HC, D], F32)
        c0b = sb("c0b", [P, HC], F32)
        c1b = sb("c1b", [P, D], F32)
        wide = sb("wide", [P, 2 * B * S], F32)

        passed = sem("passed")
        d_const = sem("d_const")
        d_ffn = sem("d_ffn")
        g_const = sem("g_const")
        g_mask = sem("g_mask")
        d_al = sem("d_al")
        v_mix = sem("v_mix")
        v_wqk = sem("v_wqk")
        p_w0 = sem("p_w0")
        d_x = sem("d_x")
        d_lnx = [sem(f"d_lnx{k}") for k in range(4)]

        chain = [0]

        def step(dve, ins):
            chain[0] += 1
            ins.then_inc(v_mix, 1)
            dve.wait_ge(v_mix, chain[0])

        def mix_start(dve):
            dve.wait_ge(d_al, 32)
            dve.wait_ge(g_mask, 12)
            for i in range(3):
                step(dve, dve.tensor_scalar(a[:, 3 * i:3 * i + 3], ar[:, :], ae[:, i:i + 1], None, ALU.mult))
            step(dve, dve.memset(c0[:, :, :], 0.0))
            step(dve, dve.memset(c1[:, :, :], 0.0))
            step(dve, dve.memset(c0b[:, :], 0.0))
            step(dve, dve.memset(c1b[:, :], 0.0))
            step(dve, dve.tensor_scalar(ema[:, :], a[0:C, :], em[:, 0:1], None, ALU.mult))
            for ij in range(9):
                step(dve, dve.tensor_scalar(hma[:, ij, :], hm[:, ij, :], a[:, ij:ij + 1], None, ALU.mult))

        def mix(dve, ij):
            i, j = ij // 3, ij % 3
            e, h = EMBED[i], RATIO[j] * EMBED[i]
            dve.tensor_scalar(c0[:, 0, 0:h], c0[:, 0, 0:h], a[0:C, ij:ij + 1], None, ALU.add)
            if i:
                upper = a[0:C, ij:ij + 1] if i == 2 else ema[:, ij:ij + 1]
                dve.tensor_scalar(c0[:, 1, 0:h], c0[:, 1, 0:h], upper, None, ALU.add)
            for k in range((h + P - 1) // P):
                dve.tensor_scalar(c1[:, k, 0:e], c1[:, k, 0:e], hma[:, ij, k:k + 1], None, ALU.add)
            dve.tensor_tensor(c0b[:, :], c0b[:, :], hma[:, ij, :], ALU.add)
            step(dve, dve.tensor_scalar(c1b[:, 0:e], c1b[:, 0:e], a[:, ij:ij + 1], None, ALU.add))

        def mix_end(dve):
            dve.wait_ge(d_ffn, 16 * 4)
            dve.tensor_tensor(w0[:, :, :], w0[:, :, :], c0[:, :, :], ALU.mult)
            dve.tensor_tensor(w1[:, :, :], w1[:, :, :], c1[:, :, :], ALU.mult)
            dve.tensor_tensor(b0[:, :], b0[:, :], c0b[:, :], ALU.mult)
            step(dve, dve.tensor_tensor(b1[:, :], b1[:, :], c1b[:, :], ALU.mult))

        with ExitStack() as ph:
            tok = sb("tok", [P, TS + LAG, D], F32, ph)
            xn = sb("xn", [P, 2, 4, D + 2], F32, ph)
            idx = sb("idx", [P, TS], I32, ph)
            keeps = sb("keeps", [P, B], F32, ph)
            keep = sb("keep", [P, 1], F32, ph)
            st = sb("st", [P, 8, 6], F32, ph)
            mv = [sb(f"mv{k}", [P, 8, 2], F32, ph) for k in range(2)]
            ve = [sb(f"ve{k}", [P, 8], F32, ph) for k in range(2)]
            rstd = [sb(f"rstd{k}", [P, 8], F32, ph) for k in range(2)]
            zero = sb("zero", [P, D], F32, ph)
            wqk_s = sb("wqk_s", [C, 2, 2 * D], F32, ph)
            wp = sb("wp", [C + 1, 2, TH * TD], F32, ph)
            wv = sb("wv", [C, 2, TH * TD], F32, ph)
            wpn = sb("wpn", [2 * TD, TH // 2, D], F32, ph)
            wo = sb("wo", [TD, TH, D], F32, ph)
            t0 = sb("t0", [TD, TH, TD], F32, ph)
            lw = sb("lw", [C, 2], F32, ph)
            lb = sb("lb", [C, 2], F32, ph)
            bcol = sb("bcol", [C, 2, C + 1], F32, ph)
            G = sb("G", [C + 1, 2, D], F32, ph)
            U = sb("U", [C, 2, TH * TD], F32, ph)
            trace = sb("trace", [TD, TH, TD], F32, ph)
            X = sb("X", [2 * TD, TH // 2, D], F32, ph)

            gath = [sem(f"gath{k}") for k in range(4)]
            d_tail = sem("d_tail")
            d_idx = sem("d_idx")
            v_st = sem("v_st")
            v_ag = sem("v_ag")
            v_var = sem("v_var")
            p_rstd = sem("p_rstd")
            v_xn = sem("v_xn")
            t_tr = sem("t_tr")
            a_ln = sem("a_ln")
            t_G = sem("t_G")
            v_ch = sem("v_ch")
            v_bcol = sem("v_bcol")
            t_bw = sem("t_bw")
            v_wp = sem("v_wp")
            t_m = sem("t_m")
            c_m = sem("c_m")

            lnx = wide[0:C, :].rearrange("p (c n) -> p c n", c=2)
            tr = [[ps[0:C, 2 * k + c, :].rearrange("p (t q) -> p t q", t=4) for c in range(2)] for k in range(2)]
            G_ps = [ps[0:C, 4, 0:D], ps[0:C + 1, 5, 0:D]]
            trace_ps = ps[0:TD, 6, :].rearrange("p (h q) -> p h q", h=TH)
            X_ps = ps[:, 0:TH // 2, 0:D]
            M_ps = ps[0:C, 4:6, 0:D]

            def tile_of(t):
                return tok[:, bass.ds(t, 1), :].rearrange("p o f -> p (o f)")

            block = ph.enter_context(nc.Block())

            @block.sync
            def _(sp):
                sp.dma_start(idx[:, :], ids).then_inc(d_idx, 16)
                for to, of in ((lw[:, :], lnw), (lb[:, :], lnb), (wp[0:C, :, :], wpT), (wv[:, :, :], wvT),
                               (wpn[:, :, :], wpN), (wo[:, :, :], woT), (t0[:, :, :], t0T), (wqk_s[:, :, :], wqk),
                               (wout_s[:, :, :], wout)):
                    sp.dma_start(to, of).then_inc(d_const, 16)
                for to, of in ((w0[:, :, :], w0T), (w1[:, :, :], w1T), (b0[:, :], bfc),
                               (b1[:, :], bproj.to_broadcast([P, D]))):
                    sp.dma_start(to, of).then_inc(d_ffn, 16)
                sp.dma_start(ae[:, :], al_e.to_broadcast([P, 3])).then_inc(d_al, 16)
                sp.dma_start(ar[:, :], al_r.to_broadcast([P, 3])).then_inc(d_al, 16)
                sp.wait_ge(gath[0], 64)
                sp.dma_start(tok[0:P - 1, TS:TS + LAG, :], tok[1:P, 0:LAG, :]).then_inc(d_tail, 16)
                sp.dma_start(tok[P - 1:P, TS:TS + LAG, :], tok[0:1, 0:LAG, :]).then_inc(d_tail, 16)
                sp.wait_ge(a_ln, 2 * NG)
                for b in range(B):
                    if b == B // 2:
                        sp.wait_ge(d_lnx[0], 64)
                        sp.dma_start(lnxb[:, :, 1:S], lnx_d[0, :, :, 0:S - 1]).then_inc(d_x, 16)
                    sp.dma_start(lnx_d[b, :, :, :], lnx[:, :, b * S:(b + 1) * S]).then_inc(d_lnx[b // 4], 16)

            @block.gpsimd
            def _(pool):
                pool.wait_ge(d_idx, 16)

                def gather(t, done):
                    pool.indirect_dma_start(out=tok[:, t, :], out_offset=None, in_=wte,
                                            in_offset=bass.IndirectOffsetOnAxis(ap=idx[:, t:t + 1], axis=0)
                                            ).then_inc(done, 16)

                for t in range(12):
                    gather(t, gath[t // 4])
                pool.memset(half[:, :], -0.5).then_inc(g_const, 1)
                pool.memset(ident[:, :], 0.0).then_inc(g_const, 1)
                pool.memset(keeps[:, :], 1.0).then_inc(g_const, 1)
                pool.memset(lnxb[:, :, 0:1], 0.0).then_inc(g_const, 1)
                pool.wait_ge(g_const, 4)
                pool.affine_select(out=ident[:, :], in_=ident[:, :], compare_op=ALU.not_equal, fill=1.0,
                                   base=0, pattern=[[-1, P]], channel_multiplier=1).then_inc(g_const, 1)
                pool.affine_select(out=keeps[:, :], in_=keeps[:, :], compare_op=ALU.not_equal, fill=0.0,
                                   base=-(CH - 1), pattern=[[-CH, B]], channel_multiplier=1).then_inc(g_const, 1)
                for r in range(NR):
                    for g in (2 * r + 3, 2 * r + 4):
                        if g < NG:
                            wait(pool, gath[g % 4], 64 * (g // 4))
                            for t in range(4 * g, 4 * (g + 1)):
                                gather(t, gath[g % 4])
                        if g % 2:
                            pool.wait_ge(v_var, r + 1)
                            pool.tensor_tensor(rstd[r % 2][:, :], ve[r % 2][:, :], half[:, :],
                                               ALU.pow).then_inc(p_rstd, 1)
                pool.memset(hm[:, :, :], 1.0).then_inc(g_mask, 1)
                pool.wait_ge(g_mask, 1)
                pool.memset(em[:, :], 1.0).then_inc(g_mask, 1)
                pool.wait_ge(g_mask, 2)
                pool.affine_select(out=em[:, :], in_=em[:, :], compare_op=ALU.is_ge, fill=0.0,
                                   base=EMBED[1] - C - 1, pattern=[[0, 1]], channel_multiplier=-1).then_inc(g_mask, 1)
                for ij in range(9):
                    pool.wait_ge(g_mask, 3 + ij)
                    pool.affine_select(out=hm[:, ij, :], in_=hm[:, ij, :], compare_op=ALU.is_ge, fill=0.0,
                                       base=RATIO[ij % 3] * EMBED[ij // 3] - 1, pattern=[[-P, HC]],
                                       channel_multiplier=-1).then_inc(g_mask, 1)

            @block.scalar
            def _(act):
                act.wait_ge(d_const, 16 * 9)
                with act.Fori(0, NG // 2) as it:
                    for k in range(2):
                        g = 2 * it + k
                        act.wait_ge(t_tr, g + 1)
                        for c in range(2):
                            view = lnx[:, c, :].rearrange("p (q t) -> p t q", t=TS)
                            act.activation(view[:, bass.ds(4 * g, 4), :], tr[k][c], ACT.Identity,
                                           scale=lw[:, c:c + 1], bias=lb[:, c:c + 1]).then_inc(a_ln, 1)
                act.wait_ge(t_m, 1)
                for i in range(2):
                    act.copy(G[0:C + i, i, :], G_ps[i]).then_inc(c_m, 1)
                act.wait_ge(t_m, 2)
                for i in range(2):
                    act.copy(U[:, i, :], ps[0:C, i, :]).then_inc(c_m, 1)
                act.wait_ge(t_m, 4)
                act.copy(X[:, :, :], X_ps).then_inc(c_m, 1)
                act.wait_ge(t_m, 5)
                act.copy(M[:, :, :], M_ps).then_inc(c_m, 1)

            @block.vector
            def _(dve):
                dve.memset(xn[:, :, :, D:D + 1], 1.0).then_inc(v_ch, 1)
                dve.memset(zero[:, :], 0.0).then_inc(v_ch, 1)
                dve.memset(bcol[:, :, :], 0.0).then_inc(v_ch, 1)
                dve.wait_ge(v_ch, 3)
                dve.wait_ge(d_const, 16 * 9)
                dve.tensor_copy(bcol[:, :, C:C + 1], lb[:, :].rearrange("p (c o) -> p c o", o=1)).then_inc(v_bcol, 1)
                dve.wait_ge(t_bw, 1)
                for c in range(2):
                    dve.tensor_scalar(wp[0:C, c, :], wp[0:C, c, :], lw[:, c:c + 1], None, ALU.mult).then_inc(v_wp, 1)
                dve.tensor_copy(wp[C:C + 1, 1, :], ps[C:C + 1, 6, :]).then_inc(v_wp, 1)
                dve.tensor_scalar(t0[:, :, :], t0[:, :, :], DECAY, None, ALU.mult).then_inc(v_wp, 1)
                dve.tensor_copy(wqk_hi[:, :, :], wqk_s[:, :, :]).then_inc(v_wqk, 1)
                dve.wait_ge(v_wqk, 1)
                dve.tensor_tensor(wqk_lo[:, :, :], wqk_s[:, :, :], wqk_hi[:, :, :].bitcast(F32),
                                  ALU.subtract).then_inc(v_wqk, 1)

                def statistics(r, k, it, i):
                    wait(dve, gath[2 * k + i], 64 * (it + 1))
                    for j in range(4):
                        dve.bn_stats(st[:, 4 * i + j, :], tile_of(8 * r + 4 * i + j)).then_inc(v_st, 1)

                def variances(r, k):
                    wait_apart(dve, v_st, 8 * r + 8, passed)
                    wait_apart(dve, v_xn, 8 * (r - 1), passed)
                    for j in range(8):
                        dve.bn_aggr(mv[k][:, j, :], st[:, j, :]).then_inc(v_ag, 1)
                    dve.wait_ge(v_ag, 8 * r + 8)
                    dve.tensor_scalar(ve[k][:, :], mv[k][:, :, 1], EPS, None, ALU.add).then_inc(v_var, 1)

                def normalise(r, k):
                    dve.wait_ge(p_rstd, r + 1)
                    for i in range(2):
                        dve.wait_ge(t_G, 2 * r + i + 1)
                        for j in range(4):
                            m = 4 * i + j
                            dve.tensor_scalar(xn[:, i, j, 0:D], tile_of(8 * r + m), mv[k][:, m, 0:1],
                                              rstd[k][:, m:m + 1], ALU.subtract, ALU.mult).then_inc(v_xn, 1)

                def pair(r, k, k_next, it_next):
                    statistics(r + 1, k_next, it_next, 0)
                    normalise(r, k)
                    statistics(r + 1, k_next, it_next, 1)
                    variances(r + 1, k_next)

                for i in range(2):
                    statistics(0, 0, 0, i)
                variances(0, 0)
                pair(0, 0, 1, 0)
                pair(1, 1, 0, 1)
                with dve.Fori(1, NR // 2 - 1) as it:
                    pair(2 * it, 0, 1, it)
                    pair(2 * it + 1, 1, 0, it + 1)
                pair(NR - 2, 0, 1, NR // 2 - 1)
                dve.wait_ge(g_const, 6)
                dve.tensor_reduce(keep[:, :], keeps[:, :], AX_X, ALU.min).then_inc(v_ch, 1)
                dve.wait_ge(v_ch, 4)
                dve.wait_ge(d_tail, 32)
                dve.tensor_scalar(tok[:, TS:TS + LAG, :], tok[:, TS:TS + LAG, :], keep[:, 0:1], None,
                                  ALU.mult).then_inc(v_ag, 4)
                normalise(NR - 1, 1)
                mix_start(dve)
                dve.wait_ge(t_m, 3)
                dve.scalar_tensor_tensor(out=trace[:, :, :], in0=trace_ps, scalar=UPDATE, in1=t0[:, :, :],
                                         op0=ALU.mult, op1=ALU.add).then_inc(c_m, 1)
                for ij in range(3):
                    mix(dve, ij)

            @block.tensor
            def _(pe):
                pe.wait_ge(v_bcol, 1)
                for c in range(2):
                    last = pe.matmul(ps[0:C + 1, 6, :], bcol[:, c, :], wp[0:C, c, :], start=(c == 0), stop=(c == 1))
                last.then_inc(t_bw, 1)
                pe.matmul(G_ps[0], zero[:, 0:C], zero[:, :], start=True, stop=False).then_inc(t_G, 1)
                pe.matmul(G_ps[1], zero[:, 0:C + 1], zero[:, :], start=True, stop=False).then_inc(t_G, 1)
                pe.wait_ge(g_const, 5)

                def group(g, k):
                    pe.wait_ge(v_xn, 4 * g + 4)
                    wait(pe, a_ln, 2 * (g - 1))
                    for c in range(2):
                        for j in range(4):
                            last = pe.transpose(tr[k][c][:, j, :], xn[:, k, j, c * C:(c + 1) * C], ident[:, :])
                    last.then_inc(t_tr, 1)
                    pe.wait_ge(v_ag, 4 * (g + 2))
                    for j in range(4):
                        later = tile_of(4 * g + j + LAG)
                        pe.matmul(G_ps[0], xn[:, k, j, 0:C], later, start=False, stop=False)
                        last = pe.matmul(G_ps[1], xn[:, k, j, C:D + 1], later, start=False, stop=False)
                    last.then_inc(t_G, 1)

                group(0, 0)
                group(1, 1)
                with pe.Fori(1, NG // 2) as it:
                    group(2 * it, 0)
                    group(2 * it + 1, 1)
                pe.matmul(G_ps[0], zero[:, 0:C], zero[:, :], start=False, stop=True)
                pe.matmul(G_ps[1], zero[:, 0:C + 1], zero[:, :], start=False, stop=True).then_inc(t_m, 1)
                pe.wait_ge(c_m, 2)
                pe.wait_ge(v_wp, 4)
                pe.wait_ge(a_ln, 2 * NG)
                for i in range(2):
                    for c in range(2):
                        last = pe.matmul(ps[0:C, i, :], G[0:C + c, c, i * C:(i + 1) * C], wp[0:C + c, c, :],
                                         start=(c == 0), stop=(c == 1))
                last.then_inc(t_m, 1)
                pe.wait_ge(c_m, 4)
                for h in range(TH):
                    for c in range(2):
                        last = pe.matmul(trace_ps[:, h, :], wv[:, c, h * TD:(h + 1) * TD],
                                         U[:, c, h * TD:(h + 1) * TD], start=(c == 0), stop=(c == 1))
                last.then_inc(t_m, 1)
                pe.wait_ge(c_m, 5)
                for h in range(TH):
                    last = pe.matmul(X_ps[TD * (h % 2):TD * (h % 2 + 1), h // 2, :], trace[:, h, :], wo[:, h, :],
                                     start=True, stop=True)
                last.then_inc(t_m, 1)
                pe.wait_ge(c_m, 6)
                for i in range(2):
                    for h in range(TH // 2):
                        last = pe.matmul(M_ps[:, i, :], wpn[:, h, i * C:(i + 1) * C], X[:, h, :],
                                         start=(h == 0), stop=(h == TH // 2 - 1))
                last.then_inc(t_m, 1)

        h0 = sb("h0", [P, NT, D], F32)
        z = y = sb("z_or_y", [P, NT, D], F32)
        st2 = sb("st2", [P, NT, 6], F32)
        mv2 = sb("mv2", [P, NT, 2], F32)
        ve2 = sb("ve2", [P, NT], F32)
        rstd2 = sb("rstd2", [P, NT], F32)
        zT_hi = sb("zT_hi", [C, 2, S], F32R)
        zT_lo = sb("zT_lo", [C, 2, S], F32R)
        x_room, rest_room = sb("x", [P, 4 * S], F32), sb("rest", [P, 4 * S], F32)
        x = x_room[0:C, :].rearrange("p (c n) -> p c n", c=4)
        rest = rest_room[0:C, :].rearrange("p (c n) -> p c n", c=4)
        part = [sb(f"part{r}", [C, 4, S], BF16) for r in range(3)]
        kaug = [sb(f"kaug{k}", [P, NT, NH, 2 * HD], F32) for k in range(2)]
        mx = sb("mx", [P, NT, NH], F32)
        mrow = [sb(f"mrow{k}", [hi - lo, 2, S], BF16) for k, (lo, hi) in enumerate(LOTS)]
        o = sb("o", [P, S], F32)
        recip = sb("recip", [P, NT, 4, 1], F32)
        at = [sb(f"at{k}", [P, NT, D], F32) for k in range(2)]
        aT = sb("aT", [C, 2, S], F32)
        q_even = sb("q_even", [P, NH, S], BF16)
        k_even = sb("k_even", [P, NH, S], BF16)
        E = wide[:, 0:16 * S].rearrange("p (u j i n) -> p u j i n", u=2, j=4, i=2)
        odd = wide[:, 16 * S:16 * S + NH * S].bitcast(BF16).rearrange("p (a h n) -> p a h n", a=2, h=NH)
        qs = [q_even[:, :, :], odd[:, 0, :, :]]
        ks = [k_even[:, :, :], odd[:, 1, :, :]]
        ROWS = ST + 2

        g_ones = sem("g_ones")
        d_h0 = sem("d_h0")
        d_pt = [sem(f"d_pt{r}") for r in range(3)]
        d_st = [sem(f"d_st{g}") for g in range(3)]
        d_m = [sem(f"d_m{k}") for k in range(2)]
        d_y = sem("d_y")
        t_h0, a_h0 = sem("t_h0"), sem("a_h0")
        v_s2, v_a2, v_v2, p_r2 = sem("v_s2"), sem("v_a2"), sem("v_v2"), sem("p_r2")
        v_z = sem("v_z")
        t_zt = sem("t_zt")
        a_zh, v_zl = sem("a_zh"), sem("v_zl")
        t_pr, a_x = sem("t_pr"), sem("a_x")
        a_hi = sem("a_hi")
        p_rest, v_mid, p_lo = sem("p_rest"), sem("v_mid"), sem("p_lo")
        t_kt, a_kt = sem("t_kt"), sem("a_kt")
        t_mx, v_mx = sem("t_mx"), sem("v_mx")
        t_mt = sem("t_mt")
        v_mh, v_m = sem("v_mh"), sem("v_m")
        t_qk, a_exp = sem("t_qk"), sem("a_exp")
        t_pv = sem("t_pv")
        a_o, t_to = sem("a_o"), sem("t_to")
        v_rc, v_nm = sem("v_rc"), sem("v_nm")
        t_at, a_at = sem("t_at"), sem("a_at")
        t_op, a_y = sem("t_op"), sem("a_y")
        mb = ps[:, 7, :]

        def tiles(room, k):
            return room[:, k * NT * D:(k + 1) * NT * D].rearrange("p (t e) -> p t e", t=NT)

        hin, yin = [tiles(rest_room, 0), tiles(wide, 0)], [tiles(rest_room, 1), tiles(wide, 1)]
        hs, fz = tiles(x_room, 0), tiles(x_room, 1)
        hb = [tiles(wide, 2 + k) for k in range(2)]
        res = [tiles(wide, 4 + k) for k in range(2)]
        act_s = [wide[:, (6 + 4 * k) * NT * D:(6 + 4 * k) * NT * D + HC * S].rearrange("p (m n) -> p m n", m=HC)
                 for k in range(2)]
        fz_hi, fz_lo = zT_hi, zT_lo
        st3 = sb("st3", [P, NT, 6], F32)
        mv3 = sb("mv3", [P, NT, 2], F32)
        ve3 = sb("ve3", [P, NT], F32)
        rstd3 = sb("rstd3", [P, NT], F32)

        f_ld = [sem(f"f_ld{k}") for k in range(2)]
        f_out = [sem(f"f_out{k}") for k in range(2)]
        f_h = sem("f_h")
        f_st, f_ag, f_var, f_rstd = sem("f_st"), sem("f_ag"), sem("f_var"), sem("f_rstd")
        f_z = sem("f_z")
        f_hb = sem("f_hb")
        f_zt = sem("f_zt")
        f_zh, f_zl = sem("f_zh"), sem("f_zl")
        f_up, f_act = sem("f_up"), sem("f_act")
        f_dn, f_res = sem("f_dn"), sem("f_res")

        def load_sums(sp, n, k):
            wait(sp, f_h, n - 1)
            for to, of in ((hin[k], h0_d), (yin[k], y_d)):
                sp.dma_start(to.rearrange("p t e -> p (t e)"),
                             of[bass.ds(n, 1), :, :].rearrange("o p m -> (o p) m")).then_inc(f_ld[k], 16)

        def ffn_variances(dve, n, k):
            dve.wait_ge(f_ld[k], 16 * (n - k) + 32)
            wait(dve, f_hb, NT * n)
            wait(dve, f_z, NT * n)
            dve.tensor_tensor(hs, hin[k], yin[k], ALU.add).then_inc(f_h, 1)
            dve.wait_ge(f_h, n + 1)
            for t in range(NT):
                dve.bn_stats(st3[:, t, :], hs[:, t, :]).then_inc(f_st, 1)
            wait_apart(dve, f_st, NT * n + NT, passed)
            for t in range(NT):
                dve.bn_aggr(mv3[:, t, :], st3[:, t, :]).then_inc(f_ag, 1)
            dve.wait_ge(f_ag, NT * n + NT)
            dve.tensor_scalar(ve3[:, :], mv3[:, :, 1], EPS, None, ALU.add).then_inc(f_var, 1)

        def ffn_deviations(pool, n):
            pool.wait_ge(f_var, n + 1)
            pool.tensor_tensor(rstd3[:, :], ve3[:, :], half[:, 0:NT], ALU.pow).then_inc(f_rstd, 1)

        def ffn_normalise(dve, n):
            dve.wait_ge(f_rstd, n + 1)
            wait(dve, f_zt, 2 * n)
            for t in range(NT):
                dve.tensor_scalar(fz[:, t, :], hs[:, t, :], mv3[:, t, 0:1], rstd3[:, t:t + 1],
                                  ALU.subtract, ALU.mult).then_inc(f_z, 1)

        def ffn_transpose(pe, n, c):
            pe.wait_ge(f_z, NT * n + NT)
            wait(pe, f_zl, 2 * n)
            for t in range(NT):
                last = pe.transpose(ps[0:C, 4 + c, t * P:(t + 1) * P], fz[:, t, c * C:(c + 1) * C], ident[:, :])
            last.then_inc(f_zt, 1)

        def ffn_high(act, n, c):
            act.wait_ge(f_zt, 2 * n + c + 1)
            wait(act, f_up, HC * n)
            act.copy(fz_hi[:, c, :], ps[0:C, 4 + c, :]).then_inc(f_zh, 1)

        def ffn_low(dve, n, c):
            dve.wait_ge(f_zh, 2 * n + c + 1)
            dve.tensor_tensor(fz_lo[:, c, :], ps[0:C, 4 + c, :], fz_hi[:, c, :].bitcast(F32),
                              ALU.subtract).then_inc(f_zl, 1)

        attention = ExitStack()
        block = attention.enter_context(nc.Block())

        @block.sync
        def _(sp):
            def load_x(n):
                wait_apart(sp, t_h0, 2 * n, passed)
                sp.dma_start(lnxb[:, :, 1:S], lnx_d[bass.ds(n, 1), :, :, 0:S - 1].rearrange("o p c t -> (o p) c t")
                             ).then_inc(d_x, 16)

            def store_h0(n):
                wait_apart(sp, a_h0, 2 * n + 2, passed)
                sp.dma_start(h0_d[bass.ds(n, 1), :, :].rearrange("o p m -> (o p) m"),
                             h0[:, :, :].rearrange("p t e -> p (t e)")).then_inc(d_h0, 16)

            def store_part(n, r):
                for g in range(3):
                    wait_apart(sp, d_st[g], 192 * n, passed)
                sp.wait_ge((a_hi, v_mid, p_lo)[r], (4, 2, 2)[r] * (n + 1))
                sp.dma_start(parts_d[r, :, :].rearrange("(c p) t -> p c t", p=C),
                             part[r][:, :, :]).then_inc(d_pt[r], 16)

            def load_stacks(n, par, g, part_no):
                wait_apart(sp, d_pt[part_no], 16 * n + 16, passed)
                wait(sp, t_qk, STEPS * (n - 2) + 8 * (g + 1))
                for which, parts, stack in ((0, QPARTS, qs[par]), (1, KPARTS, ks[par])):
                    for r in range(6):
                        if parts[r] == part_no:
                            rows = parts_d[part_no, which * D + 64 * g:which * D + 64 * (g + 1), :]
                            sp.dma_start(stack[HD * r:HD * (r + 1), 4 * g:4 * g + 4, :],
                                         rows.rearrange("(h d) t -> d h t", d=HD)).then_inc(d_st[g], 16)

            def load_max(n, par, lot):
                lo, hi = LOTS[lot]
                sp.wait_ge(v_m, 2 * n + lot + 1)
                wait(sp, t_qk, STEPS * (n - 1))
                for r in range(2):
                    sp.dma_start(qs[par][ST + r:ST + r + 1, lo:hi, :], mrow[lot][:, r, :]).then_inc(d_m[lot], 16)

            def store_y(n):
                wait_apart(sp, a_y, 2 * n + 2, passed)
                sp.dma_start(y_d[bass.ds(n, 1), :, :].rearrange("o p m -> (o p) m"),
                             y[:, :, :].rearrange("p t e -> p (t e)")).then_inc(d_y, 16)

            def sequence(b, par, ahead=True, first=False, front=True, last=False):
                load_max(b, par, 1)
                if front:
                    store_h0(b + 2)
                if ahead:
                    load_x(b + 3)
                if front:
                    store_part(b + 2, 0)
                    load_stacks(b + 2, par, 0, 0)
                if not last:
                    load_max(b + 1, 1 - par, 0)
                if front:
                    for r in (1, 2):
                        store_part(b + 2, r)
                    for r in (1, 2):
                        load_stacks(b + 2, par, 0, r)
                if not first:
                    store_y(b - 1)
                if front:
                    for g in (1, 2):
                        for r in range(3):
                            load_stacks(b + 2, par, g, r)

            store_h0(0)
            load_x(1)
            for r in range(3):
                store_part(0, r)
            for g in range(3):
                for r in range(3):
                    load_stacks(0, 0, g, r)
            store_h0(1)
            load_x(2)
            for r in range(3):
                store_part(1, r)
            for k in range(1, 4):
                sp.wait_ge(d_lnx[k], 64)
            for g in range(3):
                if g == 2:
                    load_max(0, 0, 0)
                for r in range(3):
                    load_stacks(1, 1, g, r)
            sequence(0, 0, first=True)
            sequence(1, 1)
            with sp.Fori(1, B // 2 - 2) as it:
                sequence(2 * it, 0)
                sequence(2 * it + 1, 1)
            sequence(B - 4, 0)
            sequence(B - 3, 1, ahead=False)
            sequence(B - 2, 0, ahead=False, front=False)
            sp.wait_ge(p_lo, 2 * B)
            sp.wait_ge(d_h0, 16)
            sp.wait_ge(d_y, 16)
            load_sums(sp, 0, 0)
            sequence(B - 1, 1, ahead=False, front=False, last=True)
            store_y(B - 1)
            sp.wait_ge(d_h0, 16 * B)
            sp.wait_ge(d_y, 16 * B)

        @block.gpsimd
        def _(pool):
            def norm(n):
                for i in range(2):
                    pool.wait_ge(v_v2, 2 * n + i + 1)
                    pool.tensor_tensor(rstd2[:, 2 * i:2 * i + 2], ve2[:, 2 * i:2 * i + 2], half[:, 0:2],
                                       ALU.pow).then_inc(p_r2, 1)

            def split(n):
                for w in range(2):
                    pool.wait_ge(a_hi, 4 * n + 2 * w + 2)
                    wait(pool, v_mid, 2 * n)
                    pool.tensor_tensor(rest[:, 2 * w:2 * w + 2, :], x[:, 2 * w:2 * w + 2, :],
                                       part[0][:, 2 * w:2 * w + 2, :], ALU.subtract).then_inc(p_rest, 1)
                for w in range(2):
                    pool.wait_ge(v_mid, 2 * n + w + 1)
                    wait(pool, d_pt[2], 16 * n)
                    pool.tensor_tensor(part[2][:, 2 * w:2 * w + 2, :], rest[:, 2 * w:2 * w + 2, :],
                                       part[1][:, 2 * w:2 * w + 2, :], ALU.subtract).then_inc(p_lo, 1)

            pool.memset(ks[0][ST:ROWS, :, :], 1.0).then_inc(g_ones, 1)
            for k in range(2):
                pool.wait_ge(g_ones, 1 + k)
                pool.memset(kaug[k][:, :, :, HD:2 * HD], 1.0).then_inc(g_ones, 1)
            pool.wait_ge(g_ones, 3)
            for n in range(2):
                norm(n)
                split(n)
            for k in range(4):
                pool.wait_ge(d_lnx[k], 64)
            pool.wait_ge(p_lo, 4)
            pool.memset(ks[1][ST:ROWS, :, :], 1.0).then_inc(g_ones, 1)
            pool.wait_ge(g_ones, 4)
            pool.wait_ge(v_mix, MIX_STEPS)
            pool.tensor_copy(w0_hi[:, :, :], w0[:, :, :]).then_inc(p_w0, 1)
            pool.wait_ge(p_w0, 1)
            pool.tensor_tensor(w0_lo[:, :, :], w0[:, :, :], w0_hi[:, :, :].bitcast(F32),
                               ALU.subtract).then_inc(p_w0, 1)
            norm(2)
            split(2)
            with pool.Fori(3, B) as n:
                norm(n)
                split(n)
            ffn_deviations(pool, 0)

        @block.scalar
        def _(act):
            def h0_copy(n, i, bank=7):
                act.wait_ge(t_h0, 2 * n + i + 1)
                if i == 0:
                    wait(act, v_z, NT * n)
                    wait(act, d_h0, 16 * n)
                act.copy(h0[:, 2 * i:2 * i + 2, :],
                         ps[:, bank, 0:2 * D].rearrange("p (t e) -> p t e", t=2)).then_inc(a_h0, 1)

            def zh_copy(n, c, bank=7):
                act.wait_ge(t_zt, 2 * n + c + 1)
                wait(act, t_pr, 4 * n)
                act.copy(zT_hi[:, c, :], ps[0:C, bank, :]).then_inc(a_zh, 1)

            def x_copy(n, c, bank=7):
                act.wait_ge(t_pr, 4 * n + c + 1)
                if c == 0:
                    wait(act, p_rest, 2 * n)
                    wait(act, t_kt, 2 * n)
                    wait(act, d_pt[0], 16 * n)
                act.copy(x[:, c, :], ps[0:C, bank, :]).then_inc(a_x, 1)
                act.wait_ge(a_x, 4 * n + c + 1)
                act.copy(part[0][:, c, :], x[:, c, :]).then_inc(a_hi, 1)

            def k_copy(n, par, c):
                act.wait_ge(t_kt, 2 * n + c + 1)
                wait(act, t_pv, 6 * (n - 1))
                act.copy(kaug[par][:, :, 6 * c:6 * c + 6, 0:HD],
                         mb[:, 0:NT * C].rearrange("p (t h d) -> p t h d", t=NT, h=6)).then_inc(a_kt, 1)

            def y_copy(n, i):
                act.wait_ge(t_op, 2 * n + i + 1)
                wait(act, d_y, 16 * n)
                act.copy(y[:, 2 * i:2 * i + 2, :],
                         mb[:, 0:2 * D].rearrange("p (t e) -> p t e", t=2)).then_inc(a_y, 1)

            def exp(b, s):
                u = s // 4
                act.wait_ge(t_qk, STEPS * b + s + 1)
                if s % 4 == 0:
                    wait(act, t_pv, 6 * b + u - 1)
                act.activation(E[:, u % 2, s % 4, :, :], ps[:, 2 * (s % 2):2 * (s % 2) + 2, :], ACT.Exp,
                               scale=SCALE).then_inc(a_exp, 1)

            def o_copy(n, g):
                act.wait_ge(t_pv, 6 * n + 2 * g + 2)
                wait(act, t_to, 3 * n + g)
                act.copy(o[:, :], ps[:, 6, :]).then_inc(a_o, 1)

            def aT_copy(n, c):
                act.wait_ge(t_at, 2 * n + c + 1)
                wait(act, t_op, 2 * n)
                act.copy(aT[:, c, :], mb[0:C, :]).then_inc(a_at, 1)

            def sequence(b, par, main=True, first=False, front=True, last=False):
                for s in range(STEPS):
                    if main:
                        exp(b, s)
                        if s in (VALUES_AT[1], VALUES_AT[3]):
                            o_copy(b, s // 8 - 1)
                    if s == LAST_VALUES_AT and not first:
                        o_copy(b - 1, 2)
                    if s in H0_AT and front:
                        h0_copy(b + 2, H0_AT.index(s))
                    if s in KEYS_AT and not last:
                        k_copy(b + 1, 1 - par, KEYS_AT.index(s))
                    if s in NORM_AT and front:
                        zh_copy(b + 2, NORM_AT.index(s))
                    if s in PROJECT_AT and front:
                        x_copy(b + 2, PROJECT_AT.index(s))
                    if s in HEADS_AT and not first:
                        aT_copy(b - 1, HEADS_AT.index(s))
                    if s in OUT_AT and not first:
                        y_copy(b - 1, OUT_AT.index(s))

            for i in range(2):
                h0_copy(0, i, bank=4 + i)
            for c in range(2):
                zh_copy(0, c, bank=6 + c)
            for c in range(4):
                x_copy(0, c, bank=c)
            sequence(-1, 1, main=False, first=True)
            for k in range(4):
                act.wait_ge(d_lnx[k], 64)
            sequence(0, 0, first=True)
            sequence(1, 1)
            with act.Fori(1, B // 2 - 2) as it:
                sequence(2 * it, 0)
                sequence(2 * it + 1, 1)
            sequence(B - 4, 0)
            sequence(B - 3, 1)
            sequence(B - 2, 0, front=False)
            sequence(B - 1, 1, front=False, last=True)
            o_copy(B - 1, 2)
            for c in range(2):
                aT_copy(B - 1, c)
            for i in range(2):
                y_copy(B - 1, i)
            act.wait_ge(t_pr, 4 * B)
            for c in range(2):
                ffn_high(act, 0, c)

        @block.vector
        def _(dve):
            def norm(n, i):
                dve.wait_ge(a_h0, 2 * n + i + 1)
                for t in (2 * i, 2 * i + 1):
                    dve.bn_stats(st2[:, t, :], h0[:, t, :]).then_inc(v_s2, 1)
                wait_apart(dve, v_s2, NT * n + 2 * i + 2, passed)
                for t in (2 * i, 2 * i + 1):
                    dve.bn_aggr(mv2[:, t, :], st2[:, t, :]).then_inc(v_a2, 1)
                dve.wait_ge(v_a2, NT * n + 2 * i + 2)
                dve.tensor_scalar(ve2[:, 2 * i:2 * i + 2], mv2[:, 2 * i:2 * i + 2, 1], EPS, None,
                                  ALU.add).then_inc(v_v2, 1)

            def normalise(n, i):
                dve.wait_ge(p_r2, 2 * n + i + 1)
                if i == 0:
                    wait(dve, t_zt, 2 * n)
                    wait(dve, d_y, 16 * (n - 3))
                for t in (2 * i, 2 * i + 1):
                    dve.tensor_scalar(z[:, t, :], h0[:, t, :], mv2[:, t, 0:1], rstd2[:, t:t + 1],
                                      ALU.subtract, ALU.mult).then_inc(v_z, 1)

            def z_low(n, c, bank=7):
                dve.wait_ge(a_zh, 2 * n + c + 1)
                dve.tensor_tensor(zT_lo[:, c, :], ps[0:C, bank, :], zT_hi[:, c, :].bitcast(F32),
                                  ALU.subtract).then_inc(v_zl, 1)

            def middle(n, w):
                dve.wait_ge(p_rest, 2 * n + w + 1)
                wait(dve, d_pt[1], 16 * n)
                dve.tensor_copy(part[1][:, 2 * w:2 * w + 2, :], rest[:, 2 * w:2 * w + 2, :]).then_inc(v_mid, 1)

            def maxima(n, k):
                dve.wait_ge(t_mx, MAXIMA * n + k + 1)
                if k % (8 * NT) == 0:
                    wait(dve, t_mt, 2 * n - 1 + k // (8 * NT))
                dve.tensor_reduce(mx[:, k % NT, k // NT:k // NT + 1], ps[:, 4 + k % 2, :], AX_X,
                                  ALU.max).then_inc(v_mx, 1)

            def max_rows(n, lot):
                rows, heads = mrow[lot], LOTS[lot][1] - LOTS[lot][0]
                dve.wait_ge(t_mt, 2 * n + lot + 1)
                wait(dve, d_m[lot], 32 * n)
                dve.tensor_scalar(rows[:, 0, :], mb[0:heads, :], -1.0, None, ALU.mult).then_inc(v_mh, 1)
                dve.wait_ge(v_mh, 2 * n + lot + 1)
                dve.scalar_tensor_tensor(out=rows[:, 1, :], in0=mb[0:heads, :], scalar=-1.0, in1=rows[:, 0, :],
                                         op0=ALU.mult, op1=ALU.subtract).then_inc(v_m, 1)

            def weigh(n, par, g):
                heads = mb[:, :].rearrange("p (t h c) -> p t h c", t=NT, h=4)
                dve.wait_ge(t_to, 3 * n + g + 1)
                dve.reciprocal(recip[:, :, :, :], heads[:, :, :, HD:HD + 1]).then_inc(v_rc, 1)
                dve.wait_ge(v_rc, 3 * n + g + 1)
                wait(dve, t_at, 2 * (n - 1))
                dve.tensor_tensor(at[par][:, :, 64 * g:64 * (g + 1)].rearrange("p t (h d) -> p t h d", h=4),
                                  heads[:, :, :, 0:HD], recip[:, :, :, :].to_broadcast([P, NT, 4, HD]),
                                  ALU.mult).then_inc(v_nm, 1)

            def sequence(b, par, main=True, first=False, front=True, last=False):
                k = 0
                for s in range(STEPS):
                    counts = (MAX_AT if main else MAX_ALONE)[s]
                    for place in range(5):
                        if place == 3 and s == H0_AT[1] and front:
                            norm(b + 2, 0)
                        if place == 4:
                            if s == LATE_MAX_AT and main:
                                max_rows(b, 1)
                            if s == H0_AT[1] + 1 and front:
                                norm(b + 2, 1)
                                if not main:
                                    mix_end(dve)
                                normalise(b + 2, 0)
                                normalise(b + 2, 1)
                            if s in NORM_AT and front:
                                z_low(b + 2, NORM_AT.index(s))
                            if s == LAST_SUMS_AT and not first:
                                weigh(b - 1, 1 - par, 2)
                            if s in (PROJECT_AT[1] + 2, PROJECT_AT[3] + 3) and front:
                                middle(b + 2, (s - PROJECT_AT[1]) // 3)
                            if s in SUMS_AT and main:
                                weigh(b, par, SUMS_AT.index(s))
                            if s == EARLY_MAX_AT and not last:
                                max_rows(b + 1, 0)
                        if not last:
                            for _ in range(counts[place]):
                                maxima(b + 1, k)
                                k += 1

            for ij in range(3, 5):
                mix(dve, ij)
            for i in range(2):
                norm(0, i)
            for i in range(2):
                normalise(0, i)
            for c in range(2):
                z_low(0, c, bank=6 + c)
            for ij in range(5, 8):
                mix(dve, ij)
            middle(0, 0)
            mix(dve, 8)
            middle(0, 1)
            sequence(-1, 1, main=False, first=True)
            sequence(0, 0, first=True)
            sequence(1, 1)
            with dve.Fori(1, B // 2 - 2) as it:
                sequence(2 * it, 0)
                sequence(2 * it + 1, 1)
            sequence(B - 4, 0)
            sequence(B - 3, 1)
            sequence(B - 2, 0, front=False)
            sequence(B - 1, 1, front=False, last=True)
            dve.wait_ge(t_kt, 2 * B)
            ffn_variances(dve, 0, 0)
            ffn_normalise(dve, 0)
            weigh(B - 1, 1, 2)
            for c in range(2):
                ffn_low(dve, 0, c)

        @block.tensor
        def _(pe):
            def h0_tiles(n, i, t, bank=7):
                if i == 0 and t == 0:
                    pe.wait_ge(d_x, 16 * n + 16)
                for c in range(2):
                    last = pe.matmul(ps[:, bank, t * D:(t + 1) * D],
                                     lnxb[:, c, (2 * i + t) * P:(2 * i + t + 1) * P], M[:, c, :],
                                     start=(c == 0), stop=(c == 1))
                if t == 1:
                    last.then_inc(t_h0, 1)

            def z_transpose(n, c, bank=7):
                pe.wait_ge(v_z, NT * n + NT)
                for t in range(NT):
                    last = pe.transpose(ps[0:C, bank, t * P:(t + 1) * P], z[:, t, c * C:(c + 1) * C], ident[:, :])
                last.then_inc(t_zt, 1)

            def project(n, c, k, bank=7):
                if k == 0:
                    pe.wait_ge(v_zl, 2 * n + 2)
                for j, (w, zp) in enumerate(((wqk_hi, zT_hi), (wqk_hi, zT_lo), (wqk_lo, zT_hi))):
                    last = pe.matmul(ps[0:C, bank, :], w[:, k, c * C:(c + 1) * C], zp[:, k, :],
                                     start=(k == 0 and j == 0), stop=(k == 1 and j == 2))
                if k == 1:
                    last.then_inc(t_pr, 1)

            def k_transpose(n, c):
                pe.wait_ge(a_x, 4 * n + 4)
                for t in range(NT):
                    last = pe.transpose(mb[:, t * C:(t + 1) * C], x[:, 2 + c, t * P:(t + 1) * P], ident[0:C, 0:C])
                last.then_inc(t_kt, 1)

            def max_scores(n, par, k):
                h, t = k // NT, k % NT
                if k % (4 * NT) == 0:
                    pe.wait_ge(d_st[h // 4], 192 * n + 192)
                wait(pe, v_mx, MAXIMA * n + k - 1)
                pe.matmul(ps[:, 4 + k % 2, :], qs[par][0:ST, h, t * P:(t + 1) * P], ks[par][0:ST, h, :],
                          start=True, stop=True).then_inc(t_mx, 1)

            def max_transpose(n, lot):
                lo, hi = LOTS[lot]
                pe.wait_ge(v_mx, MAXIMA * n + NT * hi)
                for t in range(NT):
                    last = pe.transpose(mb[0:hi - lo, t * P:(t + 1) * P], mx[:, t, lo:hi], ident[:, :])
                last.then_inc(t_mt, 1)

            def scores(b, par, s):
                h = 4 * (s // 8) + s % 4
                if s in (0, 16):
                    pe.wait_ge(d_m[s // 16], 32 * b + 32)
                wait(pe, a_exp, STEPS * b + s - 1)
                for i in range(2):
                    t = 2 * (s // 4 % 2) + i
                    last = pe.matmul(ps[:, 2 * (s % 2) + i, :], ks[par][0:ROWS, h, t * P:(t + 1) * P],
                                     qs[par][0:ROWS, h, :], start=True, stop=True)
                last.then_inc(t_qk, 1)

            def values(b, par, u, i):
                if i == 0:
                    if u == 0:
                        pe.wait_ge(a_kt, 2 * b + 2)
                    if u % 2 == 0:
                        wait(pe, a_o, 3 * b + u // 2)
                    pe.wait_ge(a_exp, STEPS * b + 4 * u + 4)
                t = 2 * (u % 2) + i
                for j in range(4):
                    last = pe.matmul(ps[32 * j:32 * j + 32, 6, :], kaug[par][:, t, 4 * (u // 2) + j, :],
                                     E[:, u % 2, j, i, :], start=(t == 0), stop=(t == NT - 1))
                if i == 1:
                    last.then_inc(t_pv, 1)

            def o_transpose(n, g):
                pe.wait_ge(a_o, 3 * n + g + 1)
                for t in range(NT):
                    last = pe.transpose(mb[:, t * P:(t + 1) * P], o[:, t * P:(t + 1) * P], ident[:, :])
                last.then_inc(t_to, 1)

            def a_transpose(n, par, c):
                pe.wait_ge(v_nm, 3 * n + 3)
                for t in range(NT):
                    last = pe.transpose(mb[0:C, t * P:(t + 1) * P], at[par][:, t, c * C:(c + 1) * C], ident[:, :])
                last.then_inc(t_at, 1)

            def out_tiles(n, i, t):
                if t == 0:
                    pe.wait_ge(a_at, 2 * n + 2)
                for c in range(2):
                    last = pe.matmul(mb[:, t * D:(t + 1) * D], aT[:, c, (2 * i + t) * P:(2 * i + t + 1) * P],
                                     wout_s[:, c, :], start=(c == 0), stop=(c == 1))
                if t == 1:
                    last.then_inc(t_op, 1)

            def sequence(b, par, main=True, first=False, front=True, last=False):
                k = 0
                for s in range(STEPS):
                    counts = (MAX_AT if main else MAX_ALONE)[s]

                    def max_products(place):
                        if not last:
                            for j in range(counts[place]):
                                max_scores(b + 1, 1 - par, k + sum(counts[:place]) + j)

                    if main:
                        scores(b, par, s)
                    max_products(0)
                    for i in range(2):
                        if s in VALUES_AT and main:
                            values(b, par, VALUES_AT.index(s), i)
                        if s == LAST_VALUES_AT and not first:
                            values(b - 1, 1 - par, 5, i)
                        max_products(1 + i)
                    if s == LATE_MAX_AT and main:
                        if first:
                            pe.wait_ge(v_m, 2 * b + 1)
                        else:
                            pe.wait_ge(v_nm, 3 * b - 1)
                        max_transpose(b, 1)
                    if s in H0_AT and front:
                        i = H0_AT.index(s)
                        if i == 1:
                            pe.wait_ge(a_h0, 2 * (b + 2) + 1)
                        elif main:
                            pe.wait_ge(v_m, 2 * b + 2)
                        h0_tiles(b + 2, i, 0)
                        max_products(3)
                        h0_tiles(b + 2, i, 1)
                    if s in KEYS_AT and not last:
                        if s == KEYS_AT[1]:
                            pe.wait_ge(a_kt, 2 * (b + 1) + 1)
                        elif front:
                            pe.wait_ge(a_h0, 2 * (b + 2) + 2)
                        else:
                            pe.wait_ge(v_m, 2 * b + 2)
                        k_transpose(b + 1, KEYS_AT.index(s))
                    if s in NORM_AT and front:
                        if s == NORM_AT[0]:
                            pe.wait_ge(a_kt, 2 * (b + 1) + 2)
                        else:
                            pe.wait_ge(v_zl, 2 * (b + 2) + 1)
                        z_transpose(b + 2, NORM_AT.index(s))
                    if s in PROJECT_AT and front:
                        c = PROJECT_AT.index(s)
                        if c == 1 and not first:
                            pe.wait_ge(v_nm, 3 * b)
                        elif c > 0:
                            pe.wait_ge(a_x, 4 * (b + 2) + c)
                        project(b + 2, c, 0)
                        max_products(3)
                        project(b + 2, c, 1)
                    if s == LAST_SUMS_AT and not first:
                        if front:
                            pe.wait_ge(a_x, 4 * (b + 2) + 1)
                        elif not last:
                            pe.wait_ge(a_kt, 2 * (b + 1) + 2)
                        else:
                            pe.wait_ge(v_m, 2 * b + 2)
                        o_transpose(b - 1, 2)
                    if s == SUMS_AT[0] and main:
                        if front:
                            pe.wait_ge(a_x, 4 * (b + 2) + 4)
                        else:
                            pe.wait_ge(v_nm, 3 * b)
                        o_transpose(b, 0)
                    if s in HEADS_AT and not first:
                        if s == HEADS_AT[0]:
                            pe.wait_ge(v_nm, 3 * b + 1)
                        else:
                            pe.wait_ge(a_at, 2 * b - 1)
                        a_transpose(b - 1, 1 - par, HEADS_AT.index(s))
                    if s in OUT_AT and not first:
                        i = OUT_AT.index(s)
                        if i == 0:
                            pe.wait_ge(a_at, 2 * b)
                        elif not last:
                            pe.wait_ge(v_m, 2 * b + 3)
                        else:
                            pe.wait_ge(a_y, 2 * b - 1)
                        out_tiles(b - 1, i, 0)
                        max_products(3)
                        out_tiles(b - 1, i, 1)
                    if s == EARLY_MAX_AT and not last:
                        if not main:
                            pe.wait_ge(a_x, 4 * (b + 2) + 4)
                        elif first:
                            pe.wait_ge(v_nm, 3 * b + 1)
                        else:
                            pe.wait_ge(a_y, 2 * b - 1)
                        max_transpose(b + 1, 0)
                    if s == SUMS_AT[1] and main:
                        if first:
                            pe.wait_ge(v_m, 2 * b + 3)
                        else:
                            pe.wait_ge(a_y, 2 * b)
                        o_transpose(b, 1)
                    if (s in H0_AT + PROJECT_AT and not front) or (s in OUT_AT and first):
                        max_products(3)
                    max_products(4)
                    k += sum(counts)

            for i in range(2):
                for t in range(2):
                    h0_tiles(0, i, t, bank=4 + i)
            for c in range(2):
                z_transpose(0, c, bank=6 + c)
            for c in range(4):
                for k in range(2):
                    project(0, c, k, bank=c)
            sequence(-1, 1, main=False, first=True)
            pe.wait_ge(g_ones, 4)
            sequence(0, 0, first=True)
            sequence(1, 1)
            with pe.Fori(1, B // 2 - 2) as it:
                sequence(2 * it, 0)
                sequence(2 * it + 1, 1)
            sequence(B - 4, 0)
            sequence(B - 3, 1)
            sequence(B - 2, 0, front=False)
            sequence(B - 1, 1, front=False, last=True)
            for i in range(2):
                values(B - 1, 1, 5, i)
            pe.wait_ge(v_nm, 3 * B - 1)
            o_transpose(B - 1, 2)
            for c in range(2):
                wait(pe, a_at, c and 2 * (B - 1) + 1)
                a_transpose(B - 1, 1, c)
            for i in range(2):
                wait(pe, a_y, i and 2 * (B - 1) + 1)
                for t in range(2):
                    out_tiles(B - 1, i, t)
                ffn_transpose(pe, 0, i)

        attention.close()

        block = top.enter_context(nc.Block())

        @block.sync
        def _(sp):
            def store(n, k):
                wait_apart(sp, f_res, 2 * n + 2, passed)
                sp.dma_start(out[bass.ds(n, 1), :, :].rearrange("o (t p) e -> p (o t) e", p=P),
                             res[k][:, :, :]).then_inc(f_out[k], 16)

            load_sums(sp, 1, 1)
            with sp.Fori(0, B // 2 - 1) as it:
                for k in range(2):
                    load_sums(sp, 2 * it + k + 2, k)
                    store(2 * it + k, k)
            for k in range(2):
                store(B - 2 + k, k)
            for k in range(2):
                sp.wait_ge(f_out[k], 16 * (B // 2))

        @block.gpsimd
        def _(pool):
            def residual(n, k):
                for t in range(NT):
                    pool.tensor_tensor(hb[k][:, t, :], hs[:, t, :], b1[:, :], ALU.add).then_inc(f_hb, 1)

            residual(0, 0)
            ffn_deviations(pool, 1)
            residual(1, 1)
            with pool.Fori(1, B // 2) as it:
                for k in range(2):
                    ffn_deviations(pool, 2 * it + k)
                    residual(2 * it + k, k)

        @block.scalar
        def _(act):
            def gelu(n, k, m):
                act.wait_ge(f_up, HC * n + m + 1)
                if m == 0:
                    wait(act, f_dn, 2 * (n - 1))
                act.activation(act_s[k][:, m, :], ps[:, (2 * k + m) % 4, :], ACT.Gelu_apprx_tanh,
                               bias=b0[:, m:m + 1]).then_inc(f_act, 1)

            def sequence(n, k, last=False):
                for m in range(HC):
                    gelu(n, k, m)
                if not last:
                    for c in range(2):
                        ffn_high(act, n + 1, c)

            sequence(0, 0)
            sequence(1, 1)
            with act.Fori(1, B // 2 - 1) as it:
                sequence(2 * it, 0)
                sequence(2 * it + 1, 1)
            sequence(B - 2, 0)
            sequence(B - 1, 1, last=True)

        @block.vector
        def _(dve):
            def result(n, k, i):
                dve.wait_ge(f_dn, 2 * n + i + 1)
                if i == 0:
                    dve.wait_ge(f_hb, NT * n + NT)
                    wait(dve, f_out[k], 8 * (n - k))
                dve.tensor_tensor(res[k][:, 2 * i:2 * i + 2, :],
                                  ps[:, 6 + i, 0:2 * D].rearrange("p (t e) -> p t e", t=2),
                                  hb[k][:, 2 * i:2 * i + 2, :], ALU.add).then_inc(f_res, 1)

            def sequence(n, k, last=False, norms=True):
                if not last:
                    for c in range(2):
                        ffn_low(dve, n + 1, c)
                for i in range(2):
                    result(n, k, i)
                if norms:
                    norm(n + 2, k)

            def norm(n, k):
                ffn_variances(dve, n, k)
                ffn_normalise(dve, n)

            norm(1, 1)
            sequence(0, 0)
            sequence(1, 1)
            with dve.Fori(1, B // 2 - 1) as it:
                sequence(2 * it, 0)
                sequence(2 * it + 1, 1)
            sequence(B - 2, 0, norms=False)
            sequence(B - 1, 1, last=True, norms=False)

        @block.tensor
        def _(pe):
            def up(n, k, m):
                if m == 0:
                    pe.wait_ge(f_zl, 2 * n + 2)
                wait(pe, f_act, HC * n + m - 3)
                for c in range(2):
                    for j, (w, part_z) in enumerate(((w0_hi, fz_hi), (w0_hi, fz_lo), (w0_lo, fz_hi))):
                        last = pe.matmul(ps[:, (2 * k + m) % 4, :], w[:, c, m * P:(m + 1) * P],
                                         part_z[:, c, :], start=(c == 0 and j == 0), stop=(c == 1 and j == 2))
                last.then_inc(f_up, 1)

            def down(n, k, i):
                wait(pe, f_res, 2 * (n - 1) + i + 1)
                for t in range(2):
                    for m in range(HC):
                        if i == 0 and t == 0:
                            pe.wait_ge(f_act, HC * n + m + 1)
                        last = pe.matmul(ps[:, 6 + i, t * D:(t + 1) * D],
                                         act_s[k][:, m, (2 * i + t) * P:(2 * i + t + 1) * P], w1[:, m, :],
                                         start=(m == 0), stop=(m == HC - 1))
                last.then_inc(f_dn, 1)

            def sequence(n, k, last=False):
                for m in range(HC):
                    up(n, k, m)
                    if m in (4, 5) and not last:
                        ffn_transpose(pe, n + 1, m - 4)
                for i in range(2):
                    down(n, k, i)

            sequence(0, 0)
            sequence(1, 1)
            with pe.Fori(1, B // 2 - 1) as it:
                sequence(2 * it, 0)
                sequence(2 * it + 1, 1)
            sequence(B - 2, 0)
            sequence(B - 1, 1, last=True)




def layouts(x, wte, W_proj, ln_w, ln_b, W_val, W_out, trace0, w_qkv, w_out, w_fc, b_fc, w_proj, b_proj, ae, ar):
    chunks = lambda w: np.ascontiguousarray(w.reshape(2, C, -1).transpose(1, 0, 2))
    return {
        "ids": x.reshape(B * CH, TS), "wte": wte,
        "wpT": chunks(W_proj.T), "wvT": chunks(W_val.T),
        "wpN": np.ascontiguousarray(W_proj.reshape(TH // 2, 2 * TD, D).transpose(1, 0, 2)),
        "woT": np.ascontiguousarray(W_out.T.reshape(TH, TD, D).transpose(1, 0, 2)),
        "t0T": np.ascontiguousarray(trace0.transpose(2, 0, 1)),
        "lnw": np.ascontiguousarray(ln_w.reshape(2, C).T), "lnb": np.ascontiguousarray(ln_b.reshape(2, C).T),
        "wqk": chunks(w_qkv[:, :2 * D]), "wout": chunks(w_out),
        "w0T": chunks(w_fc.T), "bfc": np.ascontiguousarray(b_fc.reshape(HC, P).T),
        "w1T": np.ascontiguousarray(w_proj.T.reshape(HC, P, D).transpose(1, 0, 2)), "bproj": b_proj.reshape(1, D),
        "al_e": ae.reshape(1, 3), "al_r": ar.reshape(1, 3),
    }


_INS = ['x', 'L0_tok_wte', 'L0_tok_W_proj', 'L0_tok_ln_w', 'L0_tok_ln_b', 'L0_tok_W_val', 'L0_tok_W_out',
        'L0_tok_trace0', 'L0_attn_w_qkv', 'L0_attn_w_out', 'L0_ffn_w_fc', 'L0_ffn_b_fc', 'L0_ffn_w_proj',
        'L0_ffn_b_proj', 'L0_ffn_alpha_e', 'L0_ffn_alpha_r']


def kernel(**inputs):
    import concourse.bacc as bacc
    from concourse.bass_utils import run_bass_kernel_spmd

    arrays = layouts(*(np.asarray(inputs[name]) for name in _INS))
    nc = bacc.Bacc("TRN2", target_bir_lowering=False, num_devices=1)
    ins = {k: nc.dram_tensor(k, v.shape, mybir.dt.from_np(v.dtype), kind="ExternalInput").ap()
           for k, v in arrays.items()}
    out = nc.dram_tensor("out", (B, S, D), F32, kind="ExternalOutput").ap()
    tower(nc, *ins.values(), out)
    r = run_bass_kernel_spmd(nc, [arrays], core_ids=[0])
    return r.results[0]["out"]
```
